# Optimizing a Trainium2 kernel written in Bass

```python
import numpy as np
import jax
import jax.numpy as jnp

def _softmax(x, axis=-1):
    return jax.nn.softmax(x, axis=axis)
def _gelu(x):
    return jax.nn.gelu(x, approximate=True)
def _silu(x):
    return jax.nn.silu(x)
def _sigmoid(x):
    return jax.nn.sigmoid(x)
def _layernorm(x, axis=-1, eps=1e-5):
    m = jnp.mean(x, axis=axis, keepdims=True)
    v = jnp.var(x, axis=axis, keepdims=True)
    return (x - m) / jnp.sqrt(v + eps)
def _scatter_add(tgt, idx, src, axis=0):
    return tgt.at[idx].add(src)
def _segment_sum(src, seg, n):
    return jax.ops.segment_sum(src, seg, n)

kernel_name = 'mk_conv_preact_d2_conv_nchw256_c469e4'

def setup_inputs(seed: int = 0):
    np.random.seed(seed)
    _w = jnp.asarray
    def _rec_inputs():
        import jax
        import jax.numpy as jnp
        _gk = jax.random.key(seed)
        x = -0.0002023 + 1 * jax.random.normal(jax.random.fold_in(_gk, 1), (32, 256, 28, 28), jnp.float32)
        return x
    x = _rec_inputs()
    def _L0_conv_setup():
        import jax, jax.numpy as jnp
        import numpy as np
        B, C_IN, H, W = (32, 256, 28, 28)
        NUM, C_OUT, K = (8, 256, 3)
        STRIDE, PAD = (1, 1)
        key = jax.random.key(seed)
        k0, k1, k2 = jax.random.split(key, 3)
        inputs = jax.random.normal(k0, (B, C_IN, H, W), dtype=jnp.float32)
        route_w = jax.random.normal(k1, (NUM, C_IN), dtype=jnp.float32) * 0.01
        route_b = jnp.zeros((NUM,), dtype=jnp.float32)
        std = float(np.sqrt(1.0 / (C_IN * K * K)))
        weight = jax.random.normal(k2, (C_OUT * C_IN * K * K, NUM), dtype=jnp.float32) * std
        bias = jnp.zeros((C_OUT,), dtype=jnp.float32)
        return {'inputs': inputs, 'route_w': route_w, 'route_b': route_b, 'weight': weight, 'bias': bias}
    _L0_conv_all = _L0_conv_setup()
    _L0_conv_in = {k: v for k, v in _L0_conv_all.items() if k in ('route_w', 'route_b', 'weight', 'bias', )}
    del _L0_conv_all

    def _L1_conv_setup():
        import jax, jax.numpy as jnp
        import numpy as np
        from jax import lax
        EPS = 1e-05

        def _feature_map(t):
            t = jax.nn.relu(t) + EPS
            t = t * t
            n = jnp.sqrt(jnp.sum(t * t, axis=1, keepdims=True))
            return t / jnp.maximum(n, 1e-12)

        def _forward(x, qkv_w, qkv_b, dwc_w, dwc_b, norm_w, proj_w, proj_b):
            B, C, H, W = x.shape
            N = H * W
            d = norm_w.shape[0]
            qkv = jnp.einsum('bchw,oc->bohw', x, qkv_w) + qkv_b[None, :, None, None]
            qkv = qkv.reshape(B, 3 * d, N)
            q, k, v = jnp.split(qkv, 3, axis=1)
            q = _feature_map(q)
            k = _feature_map(k)
            scale = N ** (-0.5)
            kmean = jnp.mean(k, axis=2)
            z = jnp.einsum('bd,bdn->bn', kmean, q)[:, None, :] + EPS
            vkT = jnp.einsum('bin,bjn->bij', v * scale, k * scale)
            attn = jnp.einsum('bij,bjn->bin', vkT, q) / z
            rms = jnp.sqrt(jnp.mean(attn * attn, axis=1, keepdims=True) + EPS)
            attn = attn / rms * norm_w[None, :, None]
            attn = attn.reshape(B, d, H, W)
            v_img = v.reshape(B, d, H, W)
            dw = lax.conv_general_dilated(v_img, dwc_w, window_strides=(1, 1), padding='SAME', feature_group_count=d, dimension_numbers=('NCHW', 'OIHW', 'NCHW'))
            dw = dw + dwc_b[None, :, None, None]
            y = attn + dw
            return jnp.einsum('bdhw,cd->bchw', y, proj_w) + proj_b[None, :, None, None]
        key = jax.random.key(seed)
        ks = jax.random.split(key, 5)
        B, C, H, W = (16, 256, 64, 64)
        d, kk = (256, 5)
        x = jax.random.normal(ks[0], (B, C, H, W), jnp.float32)
        qkv_w = jax.random.normal(ks[1], (3 * d, C), jnp.float32) * 0.02
        qkv_b = jnp.zeros((3 * d,), jnp.float32)
        dwc_w = jax.random.normal(ks[2], (d, 1, kk, kk), jnp.float32) * 0.02
        dwc_b = jnp.zeros((d,), jnp.float32)
        norm_w = jnp.ones((d,), jnp.float32)
        proj_w = jax.random.normal(ks[3], (C, d), jnp.float32) * 0.02
        proj_b = jnp.zeros((C,), jnp.float32)
        return {'x': x, 'qkv_w': qkv_w, 'qkv_b': qkv_b, 'dwc_w': dwc_w, 'dwc_b': dwc_b, 'norm_w': norm_w, 'proj_w': proj_w, 'proj_b': proj_b}
    _L1_conv_all = _L1_conv_setup()
    _L1_conv_in = {k: v for k, v in _L1_conv_all.items() if k in ('qkv_w', 'qkv_b', 'dwc_w', 'dwc_b', 'norm_w', 'proj_w', 'proj_b', )}
    del _L1_conv_all

    return {
        "x": x,
        "L0_conv_route_w": _L0_conv_in["route_w"],
        "L0_conv_route_b": _L0_conv_in["route_b"],
        "L0_conv_weight": _L0_conv_in["weight"],
        "L0_conv_bias": _L0_conv_in["bias"],
        "L1_conv_qkv_w": _L1_conv_in["qkv_w"],
        "L1_conv_qkv_b": _L1_conv_in["qkv_b"],
        "L1_conv_dwc_w": _L1_conv_in["dwc_w"],
        "L1_conv_dwc_b": _L1_conv_in["dwc_b"],
        "L1_conv_norm_w": _L1_conv_in["norm_w"],
        "L1_conv_proj_w": _L1_conv_in["proj_w"],
        "L1_conv_proj_b": _L1_conv_in["proj_b"],
    }

def reference(x, L0_conv_route_w, L0_conv_route_b, L0_conv_weight, L0_conv_bias, L1_conv_qkv_w, L1_conv_qkv_b, L1_conv_dwc_w, L1_conv_dwc_b, L1_conv_norm_w, L1_conv_proj_w, L1_conv_proj_b):
    import jax
    import jax.numpy as jnp
    def _L0_conv_ref(inputs, route_w, route_b, weight, bias):
        import jax, jax.numpy as jnp
        import numpy as np
        B, C_IN, H, W = (32, 256, 28, 28)
        NUM, C_OUT, K = (8, 256, 3)
        STRIDE, PAD = (1, 1)
        b, c, h, w = inputs.shape
        se = inputs.reshape(b, c, -1).mean(axis=-1)
        gates = jax.nn.sigmoid(se @ route_w.T + route_b)
        w_dyn = (gates @ weight.T).reshape(b, C_OUT, c, K, K)

        def conv_one(xi, wi):
            return jax.lax.conv_general_dilated(xi[None], wi, window_strides=(STRIDE, STRIDE), padding=[(PAD, PAD), (PAD, PAD)], dimension_numbers=('NCHW', 'OIHW', 'NCHW'))[0]
        out = jax.vmap(conv_one)(inputs, w_dyn)
        return out + bias.reshape(1, -1, 1, 1)

    def _L1_conv_ref(x, qkv_w, qkv_b, dwc_w, dwc_b, norm_w, proj_w, proj_b):
        import jax, jax.numpy as jnp
        import numpy as np
        from jax import lax
        EPS = 1e-05

        def _feature_map(t):
            t = jax.nn.relu(t) + EPS
            t = t * t
            n = jnp.sqrt(jnp.sum(t * t, axis=1, keepdims=True))
            return t / jnp.maximum(n, 1e-12)

        def _forward(x, qkv_w, qkv_b, dwc_w, dwc_b, norm_w, proj_w, proj_b):
            B, C, H, W = x.shape
            N = H * W
            d = norm_w.shape[0]
            qkv = jnp.einsum('bchw,oc->bohw', x, qkv_w) + qkv_b[None, :, None, None]
            qkv = qkv.reshape(B, 3 * d, N)
            q, k, v = jnp.split(qkv, 3, axis=1)
            q = _feature_map(q)
            k = _feature_map(k)
            scale = N ** (-0.5)
            kmean = jnp.mean(k, axis=2)
            z = jnp.einsum('bd,bdn->bn', kmean, q)[:, None, :] + EPS
            vkT = jnp.einsum('bin,bjn->bij', v * scale, k * scale)
            attn = jnp.einsum('bij,bjn->bin', vkT, q) / z
            rms = jnp.sqrt(jnp.mean(attn * attn, axis=1, keepdims=True) + EPS)
            attn = attn / rms * norm_w[None, :, None]
            attn = attn.reshape(B, d, H, W)
            v_img = v.reshape(B, d, H, W)
            dw = lax.conv_general_dilated(v_img, dwc_w, window_strides=(1, 1), padding='SAME', feature_group_count=d, dimension_numbers=('NCHW', 'OIHW', 'NCHW'))
            dw = dw + dwc_b[None, :, None, None]
            y = attn + dw
            return jnp.einsum('bdhw,cd->bchw', y, proj_w) + proj_b[None, :, None, None]
        return _forward(x, qkv_w, qkv_b, dwc_w, dwc_b, norm_w, proj_w, proj_b)

    def _gn(v, G=32, eps=1e-5):
        B_, C_, H_, W_ = v.shape
        g = v.reshape(B_, G, C_ // G, H_, W_)
        m = jnp.mean(g, axis=(2, 3, 4), keepdims=True)
        s = jnp.var(g, axis=(2, 3, 4), keepdims=True)
        return ((g - m) / jnp.sqrt(s + eps)).reshape(v.shape)

    def _ln_c(v, eps=1e-6):
        m = jnp.mean(v, axis=1, keepdims=True)
        s = jnp.var(v, axis=1, keepdims=True)
        return (v - m) / jnp.sqrt(s + eps)

    def _ln_t(v, eps=1e-5):
        m = jnp.mean(v, axis=-1, keepdims=True)
        s = jnp.var(v, axis=-1, keepdims=True)
        return (v - m) / jnp.sqrt(s + eps)

    def _to_tokens(v):
        B_, C_, H_, W_ = v.shape
        return v.reshape(B_, C_, H_ * W_).transpose(0, 2, 1)
    def _from_tokens(t, like):
        B_, C_, H_, W_ = like.shape
        return t.transpose(0, 2, 1).reshape(B_, C_, H_, W_)

    x = x + _L0_conv_ref(_gn(x), L0_conv_route_w, L0_conv_route_b, L0_conv_weight, L0_conv_bias)
    x = x + _L1_conv_ref(_gn(x), L1_conv_qkv_w, L1_conv_qkv_b, L1_conv_dwc_w, L1_conv_dwc_b, L1_conv_norm_w, L1_conv_proj_w, L1_conv_proj_b)
    return x


_drawn_inputs = setup_inputs


def setup_inputs(seed=0):
    import zlib

    import numpy as np

    out = dict(_drawn_inputs(seed))
    spreads = {'L0_conv_route_b': (0.0, 0.1),
     'L0_conv_bias': (0.0, 0.1),
     'L1_conv_qkv_b': (0.0, 0.1),
     'L1_conv_dwc_b': (0.0, 0.458),
     'L1_conv_norm_w': (1.0, 0.2),
     'L1_conv_proj_b': (0.0, 0.1)}
    factors = {'L0_conv_route_w': 25.99, 'L1_conv_dwc_w': 8.0}
    for name, (base, spread) in spreads.items():
        noise = np.random.default_rng([zlib.crc32(name.encode()), seed]).standard_normal(out[name].shape)
        drawn = base * np.exp(spread * noise) if base else spread * noise
        out[name] = jnp.asarray(drawn.astype(out[name].dtype))
    for name, factor in factors.items():
        out[name] = (out[name] * factor).astype(out[name].dtype)
    return out
```

```python
import concourse.bass as bass
from concourse import mybir
from contextlib import ExitStack

F32 = mybir.dt.float32
F32R = mybir.dt.float32r
F16 = mybir.dt.float16
ALU = mybir.AluOpType
ACT = mybir.ActivationFunctionType
AX = mybir.AxisListType

P = 128
B, C, IMG = 32, 256, 28
CC = C // P
N = IMG * IMG
HALF = N // 2
HR = IMG // 2
NE = 8
JB = P // NE
GS = 4
NG = B // GS
U = CC * 9
GN = 8
EPS = 1e-5
WS = 1024.0
GSC = 16.0
PAD1 = IMG + 2
KCH = [5, 4, 5, 4]
BANKS = 4
WR = 6
XR = 4
TAPS = 25
KP = 11
NB = 7
NP = N // NB
Q = N // 4
KS = 64.0
PAD2 = IMG + 4
DV_LOOP = 76


class Tally:

    def __init__(self, sem):
        self.sem, self.total, self.local, self.i, self.per = sem, 0, 0, None, 0

    def loop(self, i, per):
        self.i, self.per, self.local = i, per, 0

    def end(self, turns):
        assert self.local == self.per, (self.local, self.per)
        self.total += self.per * turns
        self.i = None

    def inc(self, ins, n=1):
        ins.then_inc(self.sem, n)
        if self.i is None:
            self.total += n
        else:
            self.local += n

    def value(self):
        return self.total if self.i is None else self.i * self.per + (self.total + self.local)


def need(eng, sem, value):
    if isinstance(value, int) and value <= 0:
        return
    eng.wait_ge(sem, value)


def mk_conv_preact(nc, x, route, wmix, consts, cols, lw, rows, l1c, dwc, wpair, x1s, out):
    xv = x.rearrange("b (c p) h w -> b p c (h w)", c=CC)
    with ExitStack() as outer:
        def keep(kind, name, shape, dt=None):
            if kind == "sem":
                return outer.enter_context(nc.semaphore(name))
            return outer.enter_context(nc.sbuf_tensor(name, shape, dt))

        cst = keep("sb", "cst", [P, P], F32)
        col = keep("sb", "col", [P, cols.shape[1]], F32)
        rs = keep("sb", "rs", [P, B * CC], F32)
        nb = keep("sb", "nb", [P, B * CC], F32)
        bdh = keep("sb", "bdh", [P, B * JB], F16)
        bdl = keep("sb", "bdl", [P, B * JB], F16)
        gavg = cst[:, 0:P]
        eps = col[:, 0:1]

        prologue(nc, xv, route, wmix, consts, cols, wpair, cst, col, gavg, eps, rs, nb, bdh, bdl)
        routed_conv(nc, xv, wpair, x1s, col, rs, nb, bdh, bdl)
        if out is not None:
            linear_attention(nc, x1s, out, lw, rows, l1c, cst, col, dwc)


def prologue(nc, xv, route, wmix, consts, cols, wpair, cst, col, gavg, eps, rs, nb, bdh, bdl):
    NCH = 2 * U
    with ExitStack() as ctx:
        sb = lambda n, s, d: ctx.enter_context(nc.sbuf_tensor(n, s, d))
        sem = lambda n: ctx.enter_context(nc.semaphore(n))
        WB = 3
        wf = sb("wf", [P, WB, 1024], F32)
        wp = sb("wp", [P, WB, 2, 1024], F16)
        xs = sb("xs", [P, XR, CC, N], F32)
        bn = sb("bn", [P, XR, CC, 2, 6], F32)
        mv = sb("mv", [P, B * CC, 2], F32)
        mt = sb("mt", [P, B * CC, 2], F32)
        tmp = sb("tmp", [P, B * CC], F32)
        tm2 = sb("tm2", [P, B * CC], F32)
        se = sb("se", [P, B, CC], F32)
        rw = sb("rw", [P, CC, P], F32)
        gate = sb("gate", [P, B], F32)
        mask = sb("mask", [P, JB], F32)
        bdf = sb("bdf", [P, B, JB], F32)
        pstat = ctx.enter_context(nc.psum_tensor("pstat", [P, 512], F32))
        pgate = ctx.enter_context(nc.psum_tensor("pgate", [P, 512], F32))
        small_in = sem("small_in")
        w_in = [sem(f"w_in{i}") for i in range(WB)]
        w_out = [sem(f"w_out{i}") for i in range(WB)]
        x_in = [sem(f"x_in{i}") for i in range(XR)]
        w_hi, w_lo = sem("w_hi"), sem("w_lo")
        stats = sem("stats")
        stat_pe, gate_pe, std_ok, gate_ok, v_step = sem("stat_pe"), sem("gate_pe"), sem("std_ok"), sem("gate_ok"), sem("v_step")
        block = ctx.enter_context(nc.Block())

        @block.sync
        def _(sp):
            sp.dma_start(cst[:, :], consts).then_inc(small_in, 16)
            sp.dma_start(col[:, :], cols).then_inc(small_in, 16)
            sp.dma_start(rw[:, :, :], route[:, 0:CC * P].rearrange("p (c m) -> p c m", c=CC)).then_inc(small_in, 16)
            sp.dma_start(mask[:, :], route[:, CC * P:CC * P + JB]).then_inc(small_in, 16)
            for n in range(max(NCH, B)):
                if n < B:
                    need(sp, stats, n - XR + 1)
                    sp.dma_start(xs[:, n % XR], xv[n]).then_inc(x_in[n % XR], 16)
                need(sp, w_lo, n - WB + 1)
                sp.dma_start(wf[:, n % WB], wmix[n]).then_inc(w_in[n % WB], 16)

        @block.gpsimd
        def _(pool):
            for n in range(NCH):
                pool.wait_ge(w_lo, n + 1)
                pool.dma_start(wpair[n], wp[:, n % WB].rearrange("p k f -> p (k f)")).then_inc(w_out[n % WB], 16)
            for k in range(WB):
                pool.wait_ge(w_out[k], 16 * len(range(k, NCH, WB)))

        @block.scalar
        def _(act):
            for n in range(NCH):
                act.wait_ge(w_in[n % WB], 16 * (n // WB + 1))
                if n >= WB:
                    act.wait_ge(w_out[n % WB], 16 * (n // WB))
                act.activation(wp[:, n % WB, 0], wf[:, n % WB], ACT.Copy, scale=WS).then_inc(w_hi, 1)
            act.wait_ge(small_in, 64)
            act.wait_ge(v_step, 5)
            act.activation(tmp[:, :], tmp[:, :], ACT.Sqrt, bias=eps).then_inc(std_ok, 1)
            act.wait_ge(gate_pe, 1)
            act.activation(gate[:, :], pgate[:, 0:B], ACT.Sigmoid, bias=col[:, 1:2]).then_inc(gate_ok, 1)

        @block.vector
        def _(dve):
            steps = Tally(v_step)

            def step(ins):
                steps.inc(ins)
                dve.wait_ge(v_step, steps.value())

            for n in range(max(NCH, B)):
                if n < B:
                    k = n % XR
                    dve.wait_ge(x_in[k], 16 * (n // XR + 1))
                    for c in range(CC):
                        for h in range(2):
                            last = dve.bn_stats(bn[:, k, c, h], xs[:, k, c, h * HALF:(h + 1) * HALF])
                    last.then_inc(stats, 1)
                dve.wait_ge(w_hi, n + 1)
                dve.scalar_tensor_tensor(wp[:, n % WB, 1], wf[:, n % WB], WS, wp[:, n % WB, 0],
                                         ALU.mult, ALU.subtract).then_inc(w_lo, 1)
                if n < B:
                    dve.wait_ge(stats, n + 1)
                    for c in range(CC):
                        last = dve.bn_aggr(mv[:, n * CC + c], bn[:, k, c])
            mean, sq = mv[:, :, 0], mv[:, :, 1]
            step(last)
            step(dve.tensor_tensor(tmp[:, :], mean, mean, ALU.mult))
            step(dve.tensor_tensor(sq, sq, tmp[:, :], ALU.add))
            dve.wait_ge(stat_pe, 1)
            step(dve.tensor_copy(mt[:, :, :], pstat[:, 0:2 * B * CC].rearrange("p (a b) -> p a b", b=2)))
            dve.tensor_tensor(tm2[:, :], mt[:, :, 0], mt[:, :, 0], ALU.mult).then_inc(stats, 1)
            dve.wait_ge(stats, B + 1)
            dve.tensor_tensor(tmp[:, :], mt[:, :, 1], tm2[:, :], ALU.subtract).then_inc(stats, 1)
            dve.wait_ge(stats, B + 2)
            step(dve.tensor_scalar(tmp[:, :], tmp[:, :], 0.0, None, ALU.max))
            dve.wait_ge(std_ok, 1)
            step(dve.reciprocal(rs[:, :], tmp[:, :]))
            step(dve.scalar_tensor_tensor(nb[:, :], mt[:, :, 0], -1.0, rs[:, :], ALU.mult, ALU.mult))
            step(dve.tensor_tensor(tm2[:, :], mean, rs[:, :], ALU.mult))
            step(dve.tensor_tensor(se[:, :, :].rearrange("p b c -> p (b c)"), tm2[:, :], nb[:, :], ALU.add))
            dve.wait_ge(gate_ok, 1)
            step(dve.tensor_tensor(bdf[:, :, :], gate[:, :].unsqueeze(2).to_broadcast([P, B, JB]),
                                   mask[:, :].unsqueeze(1).to_broadcast([P, B, JB]), ALU.mult))
            bd = bdf[:, :, :].rearrange("p b j -> p (b j)")
            step(dve.tensor_copy(bdh[:, :], bd))
            step(dve.tensor_tensor(bdl[:, :], bd, bdh[:, :], ALU.subtract))

        @block.tensor
        def _(pe):
            pe.wait_ge(small_in, 64)
            pe.wait_ge(v_step, 3)
            pe.matmul(pstat[:, 0:2 * B * CC], gavg, mv[:, :, :].rearrange("p a b -> p (a b)"),
                      start=True, stop=True).then_inc(stat_pe, 1)
            pe.wait_ge(v_step, 9)
            for c in range(CC):
                last = pe.matmul(pgate[:, 0:B], rw[:, c], se[:, :, c], start=(c == 0), stop=(c == CC - 1))
            last.then_inc(gate_pe, 1)


def routed_conv(nc, xv, wpair, x1s, col, rs, nb, bdh, bdl):
    with ExitStack() as ctx:
        sb = lambda n, s, d: ctx.enter_context(nc.sbuf_tensor(n, s, d))
        sem = lambda n: ctx.enter_context(nc.semaphore(n))
        wdh = sb("wdh", [P, 2, GS, U, P], F16)
        wdl = sb("wdl", [P, 2, GS, U, P], F16)
        wr = sb("wr", [P, WR, 2, 1024], F16)
        xg = sb("xg", [P, GS, CC, N], F32)
        xh = sb("xh", [P, GS, CC, PAD1, PAD1], F16)
        xl = sb("xl", [P, GS, CC, PAD1, PAD1], F16)
        xf = sb("xf", [P, CC, N], F32)
        bg = sb("bg", [P, 2, GS * JB], F16)
        pm = [ctx.enter_context(nc.psum_tensor(f"pm{k}", [P, 512], F32)) for k in range(4)]
        pc = [ctx.enter_context(nc.psum_tensor(f"pc{k}", [P, 512], F32)) for k in range(4)]
        w_in = [sem(f"wr_in{k}") for k in range(WR)]
        x_in = [sem(f"xg_in{k}") for k in range(GS)]
        x1_out = [sem(f"x1_out{k}") for k in range(GS)]
        mixed, mix_hi, mix_lo = sem("mixed"), sem("mix_hi"), sem("mix_lo")
        conv_done, conv_out = sem("conv_done"), sem("conv_out")
        bg_ok, xf_ok, xh_ok, xl_ok, xb_ok = sem("bg_ok"), sem("xf_ok"), sem("xh_ok"), sem("xl_ok"), sem("xb_ok")
        block = ctx.enter_context(nc.Block())

        def over_groups(eng, body):
            with eng.Fori(0, NG - 1) as g:
                body(g, False)
            body(NG - 1, True)

        def chunk(g, H, u):
            return 36 * g + 18 * H + u

        def job(g, H, i):
            return 16 * g + 8 * H + 2 * i

        def chunks(H, i):
            first = sum(KCH[:i])
            return range(first, first + KCH[i])

        @block.sync
        def _(sp):
            def load_w(g, H, u):
                n = chunk(g, H, u)
                need(sp, mixed, n - WR + 1)
                sp.dma_start(wr[:, u % WR].rearrange("p k f -> p (k f)"), wpair[U * H + u]).then_inc(w_in[u % WR], 16)

            def load_x(g, i):
                if not isinstance(g, int) or g:
                    sp.wait_ge(x1_out[i], 32 * g)
                s = GS * g + i
                src = xv[s] if isinstance(s, int) else xv[bass.ds(s, 1)].rearrange("a p c n -> (a p) c n")
                sp.dma_start(xg[:, i], src).then_inc(x_in[i], 16)

            def store(g, H, i):
                sp.wait_ge(conv_out, BANKS + job(g, H, i) + 2)
                s = GS * g + i
                dst = x1s[s, H] if isinstance(s, int) else x1s[bass.ds(s, 1), H].rearrange("a p n -> (a p) n")
                sp.dma_start(dst, xg[:, i, H]).then_inc(x1_out[i], 16)

            for i in range(GS):
                load_x(0, i)
            for u in range(U):
                load_w(0, 0, u)

            def body(g, last):
                for H in range(2):
                    for i in range(GS):
                        if not (last and H):
                            for u in chunks(H, i):
                                load_w(g + H, 1 - H, u)
                        if i:
                            store(g, H, i - 1)
                        if H and not last and i:
                            load_x(g + 1, i - 1)
                    store(g, H, GS - 1)
                if not last:
                    load_x(g + 1, GS - 1)

            over_groups(sp, body)
            for i in range(GS):
                sp.wait_ge(x1_out[i], 32 * NG)

        @block.gpsimd
        def _(pool):
            def low(g, i):
                s = GS * g + i
                for c in range(CC):
                    pool.wait_ge(xh_ok, 2 * s + c + 1)
                    pool.tensor_tensor(xl[:, i, c, 1:1 + IMG, 1:1 + IMG],
                                       xf[:, c].rearrange("p (a b) -> p a b", a=IMG),
                                       xh[:, i, c, 1:1 + IMG, 1:1 + IMG], ALU.subtract).then_inc(xl_ok, 1)

            for i in range(GS):
                low(0, i)

            def body(g, last):
                for H in range(2):
                    for i in range(GS):
                        if H and not last and i:
                            low(g + 1, i - 1)
                if not last:
                    low(g + 1, GS - 1)

            over_groups(pool, body)

        @block.scalar
        def _(act):
            def high(g, i):
                s = GS * g + i
                act.wait_ge(x_in[i], 16 * g + 16)
                if isinstance(g, int) and g == 0:
                    act.wait_ge(conv_out, BANKS)
                for c in range(CC):
                    need(act, xl_ok, 2 * s + c - 1)
                    k = CC * s + c
                    sc = rs[:, k:k + 1] if isinstance(k, int) else rs[:, bass.ds(k, 1)]
                    bi = nb[:, k:k + 1] if isinstance(k, int) else nb[:, bass.ds(k, 1)]
                    act.activation(xf[:, c], xg[:, i, c], ACT.Identity, scale=sc, bias=bi).then_inc(xf_ok, 1)
                for c in range(CC):
                    act.wait_ge(xf_ok, 2 * s + c + 1)
                    act.activation(xh[:, i, c, 1:1 + IMG, 1:1 + IMG],
                                   xf[:, c].rearrange("p (a b) -> p a b", a=IMG), ACT.Copy).then_inc(xh_ok, 1)
                for c in range(CC):
                    act.activation(xg[:, i, c], xg[:, i, c], ACT.Identity, bias=col[:, 2 + c:3 + c]).then_inc(xb_ok, 1)

            def mix(g, H, u):
                n = chunk(g, H, u)
                act.wait_ge(mixed, n + 1)
                act.activation(wdh[:, H, :, u, :], pm[(2 * H + u) % 4][:, :].rearrange("p (b m) -> p b m", b=GS),
                               ACT.Copy, scale=1.0 / GSC).then_inc(mix_hi, 1)

            def gates(g):
                if not (isinstance(g, int) and g == 0):
                    act.wait_ge(mixed, 36 * g)
                for k, src in enumerate((bdh, bdl)):
                    part = src[:, 0:GS * JB] if isinstance(g, int) and g == 0 else src[:, bass.ds(GS * JB * g, GS * JB)]
                    act.activation(bg[:, k], part, ACT.Copy).then_inc(bg_ok, 1)

            gates(0)
            high(0, 0)
            for u in range(U):
                mix(0, 0, u)
            for i in range(1, GS):
                high(0, i)

            def body(g, last):
                for H in range(2):
                    if H and not last:
                        gates(g + 1)
                    for i in range(GS):
                        if not (last and H):
                            for u in chunks(H, i):
                                mix(g + H, 1 - H, u)
                        if H and not last and i:
                            high(g + 1, i - 1)
                if not last:
                    high(g + 1, GS - 1)

            over_groups(act, body)

        @block.vector
        def _(dve):
            for tile in (xh, xl):
                for i in range(0, GS, 2):
                    dve.memset(tile[:, i:i + 2], 0.0).then_inc(conv_out, 1)

            def mix(g, H, u):
                n = chunk(g, H, u)
                dve.wait_ge(mix_hi, n + 1)
                dve.scalar_tensor_tensor(wdl[:, H, :, u, :], pm[(2 * H + u) % 4][:, :].rearrange("p (b m) -> p b m", b=GS),
                                         1.0 / GSC, wdh[:, H, :, u, :], ALU.mult, ALU.subtract).then_inc(mix_lo, 1)

            def add(g, H, i):
                if H == 0:
                    dve.wait_ge(xb_ok, 2 * (GS * g + i) + 2)
                for h in range(2):
                    dve.wait_ge(conv_done, job(g, H, i) + h + 1)
                    part = xg[:, i, H, h * HALF:(h + 1) * HALF]
                    dve.scalar_tensor_tensor(part, pc[(2 * i + h) % 4][:, 0:HALF], 1.0 / WS, part,
                                             ALU.mult, ALU.add).then_inc(conv_out, 1)

            for u in range(U):
                mix(0, 0, u)

            def body(g, last):
                for H in range(2):
                    for i in range(GS):
                        if not (last and H):
                            for u in chunks(H, i):
                                mix(g + H, 1 - H, u)
                        add(g, H, i)

            over_groups(dve, body)

        @block.tensor
        def _(pe):
            def mix(g, H, u):
                n = chunk(g, H, u)
                if u == 0 and H == 0:
                    pe.wait_ge(bg_ok, 2 * g + 2)
                pe.wait_ge(w_in[u % WR], 16 * (6 * g + 3 * H + u // WR + 1))
                need(pe, mix_lo, n - 3)
                bank = pm[(2 * H + u) % 4][:, :].rearrange("p (b m) -> p b m", b=GS)
                for jb in range(8):
                    dst = bank[:, :, jb * JB:(jb + 1) * JB]
                    for k, (wk, gk) in enumerate(((0, 0), (0, 1), (1, 0))):
                        last = pe.matmul(dst, wr[:, u % WR, wk, jb * P:(jb + 1) * P],
                                         bg[:, gk].rearrange("p (b j) -> p b j", b=GS),
                                         start=(k == 0 and jb == 0), stop=(k == 2), skip_group_check=True)
                last.then_inc(mixed, 1)

            def conv(g, H, i, after):
                pe.wait_ge(mix_lo, 36 * g + 18 * H + 18)
                pe.wait_ge(xl_ok, 2 * (GS * g + i) + 2)
                pe.wait_ge(conv_out, job(g, H, i) + BANKS - 2)
                for u in range(U):
                    c, t = divmod(u, 9)
                    dy, dx = divmod(t, 3)
                    for wk, xk in ((wdh, xh), (wdh, xl), (wdl, xh)):
                        for h in range(2):
                            q = pe.matmul(pc[(2 * i + h) % 4][:, 0:HALF], wk[:, H, i, u, :],
                                          xk[:, i, c, h * HR + dy:h * HR + dy + HR, dx:dx + IMG],
                                          start=(u == 0 and wk is wdh and xk is xh), stop=(u == U - 1 and wk is wdl))
                            if u == U - 1 and wk is wdl:
                                q.then_inc(conv_done, 1)
                    if u in after:
                        mix(*after[u])

            for u in range(U):
                mix(0, 0, u)

            def body(g, last):
                for H in range(2):
                    for i in range(GS):
                        after = {}
                        if not (last and H):
                            for k, u in enumerate(chunks(H, i)):
                                after[3 * k + 2] = (g + H, 1 - H, u)
                        conv(g, H, i, after)

            over_groups(pe, body)


def linear_attention(nc, x1s, out, lw, rows, l1c, cst, col, dwc):
    ov = out.rearrange("b (c p) h w -> b p c (h w)", c=CC)
    eps, gavg = col[:, 0:1], cst[:, 0:P]
    with ExitStack() as ctx:
        sb = lambda n, s, d=F32: ctx.enter_context(nc.sbuf_tensor(n, s, d))
        sem = lambda n: ctx.enter_context(nc.semaphore(n))
        wf = sb("wf1", [P, CC, 4 * C])
        wh = sb("wh", [P, CC, 4 * C], F16)
        wl = sb("wl", [P, CC, 4 * C], F16)
        bkb = sb("bkb", [P, 2 * C])
        kc = sb("kc", [P, 6 * P])
        dr = sb("dr", [P, CC, TAPS])
        dw = sb("dw", [P, CC, TAPS])
        dgf = sb("dgf", [P, P])
        dgh = sb("dgh", [P, CC, KP, P], F16)
        dgl = sb("dgl", [P, CC, KP, P], F16)
        pbc = sb("pbc", [P, CC])
        xb = sb("xb", [P, 2, CC, N])
        bn = sb("bn1", [P, CC, 2, 6])
        mv = sb("mv1", [P, CC, 2])
        mt = sb("mt1", [P, CC, 2])
        t1 = sb("t11", [P, CC])
        t2 = sb("t12", [P, CC])
        sd = sb("sd1", [P, CC])
        r1 = sb("r11", [P, CC])
        n1 = sb("n11", [P, CC])
        hf = sb("hf", [P, CC, N])
        hh = sb("hh", [P, 2, CC, N], F16)
        hl = sb("hl", [P, 2, CC, N], F16)
        kf = sb("kf", [NP, NB, C])
        ks = sb("ks", [NP, NB, C])
        kq = sb("kq", [NP, NB])
        kn = sb("kn", [NP, NB])
        kr = sb("kr", [NP, NB])
        kh = sb("kh", [NP, NB, C], F16)
        kl = sb("kl", [NP, NB, C], F16)
        vth = sb("vth", [NP, NB, C + 2], F16)
        vtl = sb("vtl", [NP, NB, C + 2], F16)
        vk = sb("vk", [P, CC, C])
        vkh = sb("vkh", [P, CC, C], F32R)
        vkl = sb("vkl", [P, CC, C], F32R)
        km = sb("km", [P, CC])
        kmb = sb("kmb", [P, CC, 32])
        tf = sb("tf", [P, CC, N])
        th = sb("th", [P, CC, N], F32R)
        tl = sb("tl", [P, CC, N], F32R)
        sq = sb("sq", [P, CC, N])
        af = sb("af", [P, CC, N])
        nn = sb("nn", [P, Q])
        ww = sb("ww", [P, Q])
        sf = sb("sf", [P, Q])
        vp = sb("vp", [P, 2, CC, PAD2, PAD2])
        vh = sb("vh", [P, CC, PAD2, PAD2], F16)
        vl = sb("vl", [P, CC, PAD2, PAD2], F16)
        acc = sb("acc", [P, CC, N])
        yh = sb("yh", [P, CC, N], F16)
        yl = sb("yl", [P, CC, N], F16)
        of = sb("of", [P, CC, N])
        xr = sb("xr", [P, 2, CC, N])

        sl = kc[:, 0:4 * P].rearrange("p (q m) -> p q m", q=4)
        idn = kc[:, 4 * P:5 * P]
        ones, mean_ch, mean_px = kc[:, 5 * P:5 * P + 32], kc[:, 5 * P + 32:5 * P + 64], kc[:, 5 * P + 64:5 * P + 96]
        psum = lambda n: ctx.enter_context(nc.psum_tensor(n, [P, 512], F32))
        pa, pd, pb = [psum(f"pa{k}") for k in range(4)], [psum(f"pd{k}") for k in range(2)], [psum(f"pb{k}") for k in range(2)]
        a_full, a_free = [sem(f"a_full{k}") for k in range(4)], [sem(f"a_free{k}") for k in range(4)]
        d_full, d_free = [sem(f"d_full{k}") for k in range(2)], [sem(f"d_free{k}") for k in range(2)]
        b_full, b_free = [sem(f"b_full{k}") for k in range(2)], [sem(f"b_free{k}") for k in range(2)]
        w_in, w_hi, w_ok, pad_ok, dw_ok, dg_f, dg_h, pb_ok = [sem("l1_" + n) for n in (
            "w_in", "w_hi", "w_ok", "pad_ok", "dw_ok", "dg_f", "dg_h", "pb_ok")]
        xb_in, xr_in, o_out = [[sem(f"{n}{k}") for k in range(2)] for n in ("xb_in", "xr_in", "o_out")]
        bn_ok, mv_ok, sd_ok, rn_ok, hf_ok, hh_ok, hl_ok = [sem(n) for n in ("bn_ok", "mv_ok", "sd_ok", "rn_ok", "hf_ok", "hh_ok", "hl_ok")]
        vt_hi, kv_out, kf_ok, ksq_ok, kq_ok, kn_ok, kx_ok, kh_ok, kl_ok = [sem(n) for n in (
            "vt_hi", "kv_out", "kf_ok", "ksq_ok", "kq_ok", "kn_ok", "kx_ok", "kh_ok", "kl_ok")]
        vp_ok, vh_ok, vl_ok = [sem(n) for n in ("vp_ok", "vh_ok", "vl_ok")]
        qr_ok, tf_ok, th_ok, tsq_ok, tl_ok = [sem(n) for n in ("qr_ok", "tf_ok", "th_ok", "tsq_ok", "tl_ok")]
        vk_ok, vkh_ok, kmb_ok, vkl_ok = [sem(n) for n in ("vk_ok", "vkh_ok", "kmb_ok", "vkl_ok")]
        af_ok, asq_ok, nn_ok, ww_ok, fs_ok, sf_ok = [sem(n) for n in ("af_ok", "asq_ok", "nn_ok", "ww_ok", "fs_ok", "sf_ok")]
        y_ok, yh_ok, yl_ok, of_ok, o_ok, dv = [sem(n) for n in ("y_ok", "yh_ok", "yl_ok", "of_ok", "o_ok", "dv")]
        block = ctx.enter_context(nc.Block())

        KV, V, QJ, VK, SS, KZ, AT, A2 = 0, 7, 11, 15, 17, 18, 19, 23
        A = lambda s, off: (off % 4, 6 * s + off // 4)
        D = lambda s, off: (off % 2, 3 * s + 1 + off // 2 - (isinstance(s, int) and s == B - 1 and off > 3))
        BJ = lambda s, off: (off % 2, 3 * s + off // 2)

        def stat_job(s, c):
            return (c, 0) if isinstance(s, int) and s == 0 else D(s - 1, 2 + c)

        def full(eng, sems, job):
            eng.wait_ge(sems[job[0]], job[1] + 1)

        def free(eng, sems, job):
            need(eng, sems[job[0]], job[1])

        def slots(eng, slot):
            slot(0, 0, 0, "first")
            slot(1, 1, 0, "")
            slot(2, 0, 1, "")
            with eng.Fori(1, B // 2 - 1) as t:
                slot(2 * t + 1, 1, t, "")
                slot(2 * t + 2, 0, t + 1, "")
            slot(B - 1, 1, B // 2 - 1, "last")
            slot(B, 0, B // 2, "rest")

        def image(dram, s):
            if isinstance(s, int):
                return dram[s]
            return dram[bass.ds(s, 1)].rearrange("a p c n -> (a p) c n")

        x1v = x1s.rearrange("b c p n -> b p c n")

        @block.sync
        def _(sp):
            for dst, src in ((wf[:, :, :], lw), (bkb[:, :], rows), (kc[:, :], l1c), (dr[:, :, :], dwc)):
                sp.dma_start(dst, src).then_inc(w_in, 16)

            def load(s, par):
                if not (isinstance(s, int) and s < 2):
                    sp.wait_ge(hf_ok, s - 1)
                sp.dma_start(xb[:, par], image(x1v, s)).then_inc(xb_in[par], 16)

            def slot(s, par, half, kind):
                if kind in ("first", ""):
                    load(s + 1, 1 - par)
                if kind != "first":
                    r, rp = s - 1, 1 - par
                    rh = half if par else half - 1
                    if not (isinstance(s, int) and s < 3):
                        need(sp, o_out[rp], 16 * rh)
                    sp.dma_start(xr[:, rp], image(x1v, r)).then_inc(xr_in[rp], 16)
                    sp.wait_ge(o_ok, CC * (r + 1))
                    sp.dma_start(image(ov, r), xr[:, rp]).then_inc(o_out[rp], 16)

            load(0, 0)
            slots(sp, slot)
            for k in range(2):
                sp.wait_ge(o_out[k], 16 * (B // 2))

        @block.gpsimd
        def _(pool):
            def norm_low(s, par):
                pool.wait_ge(hh_ok, s + 1)
                for c in range(CC):
                    last = pool.tensor_tensor(hl[:, par, c], hf[:, c], hh[:, par, c], ALU.subtract)
                last.then_inc(hl_ok, 1)

            def v_low(s, par):
                pool.wait_ge(vh_ok, s + 1)
                for c in range(CC):
                    pool.tensor_tensor(vl[:, c, 2:2 + IMG, 2:2 + IMG], vp[:, par, c, 2:2 + IMG, 2:2 + IMG],
                                       vh[:, c, 2:2 + IMG, 2:2 + IMG], ALU.subtract).then_inc(vl_ok, 1)

            def residual(r, rp, rh):
                pool.wait_ge(xr_in[rp], 16 * (rh + 1))
                for c in range(CC):
                    pool.wait_ge(of_ok, 4 * r + 2 * c + 2)
                    pool.tensor_tensor(xr[:, rp, c], xr[:, rp, c], of[:, c], ALU.add).then_inc(o_ok, 1)

            pool.wait_ge(pad_ok, 4)
            norm_low(0, 0)

            def slot(s, par, half, kind):
                if kind != "rest":
                    v_low(s, par)
                if kind in ("first", ""):
                    norm_low(s + 1, 1 - par)
                if kind != "first":
                    residual(s - 1, 1 - par, half if par else half - 1)

            slots(pool, slot)

        @block.scalar
        def _(act):
            def norm(s, par, half):
                act.wait_ge(mv_ok, 2 * s + 1)
                act.activation(sd[:, :], sd[:, :], ACT.Sqrt, bias=eps).then_inc(sd_ok, 1)
                act.wait_ge(mv_ok, 2 * s + 2)
                need(act, hl_ok, s)
                for c in range(CC):
                    last = act.activation(hf[:, c], xb[:, par, c], ACT.Identity, scale=r1[:, c:c + 1], bias=n1[:, c:c + 1])
                last.then_inc(hf_ok, 1)
                act.wait_ge(hf_ok, s + 1)
                act.activation(hh[:, par], hf[:, :, :], ACT.Copy).then_inc(hh_ok, 1)

            def v_pixels(s, j):
                job = A(s, KV + j)
                full(act, a_full, job)
                act.activation(vth[:, j, 0:C], pa[job[0]][0:NP, C:2 * C], ACT.Copy, scale=1.0 / WS).then_inc(vt_hi, 1)

            def keys(s):
                act.wait_ge(kf_ok, s + 1)
                act.activation(kf[:, :, :], kf[:, :, :], ACT.Square).then_inc(ksq_ok, 1)
                act.wait_ge(ksq_ok, s + 1)
                for j in range(NB):
                    act.activation(ks[:, j], kf[:, j], ACT.Square, accum_out=kq[:, j:j + 1]).then_inc(kq_ok, 1)
                act.wait_ge(kq_ok, NB * s + NB)
                act.activation(kn[:, :], kq[:, :], ACT.Sqrt).then_inc(kn_ok, 1)

            def keys_high(s):
                act.wait_ge(kx_ok, s + 1)
                act.activation(kh[:, :, :], kf[:, :, :], ACT.Copy).then_inc(kh_ok, 1)

            def values(s, par):
                need(act, y_ok, s - 1)
                for c in range(CC):
                    for h in range(2):
                        job = A(s, V + 2 * c + h)
                        full(act, a_full, job)
                        act.activation(vp[:, par, c, 2 + h * HR:2 + h * HR + HR, 2:2 + IMG],
                                       pa[job[0]][:, 0:HALF].rearrange("p (a b) -> p a b", a=HR), ACT.Identity,
                                       scale=1.0 / WS, bias=col[:, 6 + c:7 + c]).then_inc(a_free[job[0]], 1)
                        act.wait_ge(a_free[job[0]], job[1] + 1)
                if not (isinstance(s, int) and s == 0):
                    full(act, d_full, D(s - 1, 5))
                for c in range(CC):
                    last = act.activation(vh[:, c, 2:2 + IMG, 2:2 + IMG], vp[:, par, c, 2:2 + IMG, 2:2 + IMG], ACT.Copy)
                last.then_inc(vh_ok, 1)

            def queries(s):
                for c in range(CC):
                    for h in range(2):
                        job = A(s, QJ + 2 * c + h)
                        full(act, a_full, job)
                        act.activation(tf[:, c, h * HALF:(h + 1) * HALF], pa[job[0]][:, 0:HALF], ACT.Relu,
                                       scale=1.0 / WS, bias=col[:, 4 + c:5 + c]).then_inc(a_free[job[0]], 1)
                        act.wait_ge(a_free[job[0]], job[1] + 1)
                act.activation(tf[:, :, :], tf[:, :, :], ACT.Square, bias=eps).then_inc(tf_ok, 1)
                act.wait_ge(tf_ok, s + 1)
                act.activation(th[:, :, :], tf[:, :, :], ACT.Copy).then_inc(th_ok, 1)
                act.activation(sq[:, :, :], tf[:, :, :], ACT.Square).then_inc(tsq_ok, 1)

            def product_high(s):
                for c in range(CC):
                    act.wait_ge(vk_ok, CC * s + c + 1)
                    act.activation(vkh[:, c], vk[:, c], ACT.Copy, scale=1.0 / (KS * N)).then_inc(vkh_ok, 1)
                    act.activation(kmb[:, c], mean_px, ACT.Copy, scale=km[:, c:c + 1]).then_inc(kmb_ok, 1)

            def attention(s):
                full(act, a_full, A(s, SS))
                act.activation(nn[:, :], pa[SS % 4][:, 0:Q], ACT.Sqrt).then_inc(a_free[SS % 4], 1)
                need(act, y_ok, s)
                for c in range(CC):
                    for h in range(2):
                        job = A(s, AT + 2 * c + h)
                        full(act, a_full, job)
                        act.activation(af[:, c, h * HALF:(h + 1) * HALF], pa[job[0]][:, 0:HALF],
                                       ACT.Copy).then_inc(a_free[job[0]], 1)
                        act.wait_ge(a_free[job[0]], job[1] + 1)
                act.activation(sq[:, :, :], af[:, :, :], ACT.Square).then_inc(asq_ok, 1)

            def scale(s):
                act.wait_ge(ww_ok, s + 1)
                act.activation(ww[:, :], ww[:, :], ACT.Sqrt).then_inc(fs_ok, 1)

            def y_high(r):
                act.wait_ge(y_ok, r + 1)
                act.activation(yh[:, :, :], acc[:, :, :], ACT.Copy).then_inc(yh_ok, 1)

            def project(r):
                need(act, o_ok, CC * r)
                for c in range(CC):
                    for h in range(2):
                        job = BJ(r, 2 + 2 * c + h)
                        full(act, b_full, job)
                        act.activation(of[:, c, h * HALF:(h + 1) * HALF], pb[job[0]][:, 0:HALF], ACT.Identity,
                                       scale=1.0 / WS, bias=pbc[:, c:c + 1]).then_inc(b_free[job[0]], 1)
                        act.wait_ge(b_free[job[0]], job[1] + 1)
                    act.nop().then_inc(of_ok, 2)

            act.wait_ge(w_in, 64)
            act.activation(wh[:, :, :], wf[:, :, :], ACT.Copy, scale=WS).then_inc(w_hi, 1)
            act.wait_ge(pad_ok, 4)
            norm(0, 0, 0)

            def slot(s, par, half, kind):
                live = kind != "rest"
                if live:
                    for j in range(NB):
                        v_pixels(s, j)
                    values(s, par)
                    queries(s)
                    keys(s)
                    keys_high(s)
                if kind != "first":
                    y_high(s - 1)
                if live:
                    product_high(s)
                if kind != "first":
                    project(s - 1)
                if kind in ("first", ""):
                    norm(s + 1, 1 - par, None)
                if live:
                    attention(s)
                    scale(s)

            slots(act, slot)

        @block.vector
        def _(dve):
            chain = Tally(dv)

            def step(ins):
                chain.inc(ins)
                dve.wait_ge(dv, chain.value())

            def moments(s, par, half):
                dve.wait_ge(xb_in[par], 16 * (half + 1))
                for c in range(CC):
                    for h in range(2):
                        last = dve.bn_stats(bn[:, c, h], xb[:, par, c, h * HALF:(h + 1) * HALF])
                step(last)
                dve.nop().then_inc(bn_ok, 1)
                for c in range(CC):
                    last = dve.bn_aggr(mv[:, c], bn[:, c])
                step(last)
                step(dve.tensor_tensor(t1[:, :], mv[:, :, 0], mv[:, :, 0], ALU.mult))
                dve.tensor_tensor(mv[:, :, 1], mv[:, :, 1], t1[:, :], ALU.add).then_inc(rn_ok, 1)

            def statistics(s):
                for c in range(CC):
                    job = stat_job(s, c)
                    full(dve, d_full, job)
                    dve.tensor_copy(mt[:, c], pd[job[0]][:, 0:2]).then_inc(d_free[job[0]], 1)
                    dve.wait_ge(d_free[job[0]], job[1] + 1)
                step(dve.tensor_tensor(t2[:, :], mt[:, :, 0], mt[:, :, 0], ALU.mult))
                step(dve.tensor_tensor(sd[:, :], mt[:, :, 1], t2[:, :], ALU.subtract))
                dve.tensor_scalar(sd[:, :], sd[:, :], 0.0, None, ALU.max).then_inc(mv_ok, 1)
                dve.wait_ge(sd_ok, s + 1)
                step(dve.reciprocal(r1[:, :], sd[:, :]))
                dve.scalar_tensor_tensor(n1[:, :], mt[:, :, 0], -1.0, r1[:, :], ALU.mult, ALU.mult).then_inc(mv_ok, 1)

            def pixels(s, j):
                job = A(s, KV + j)
                dve.wait_ge(vt_hi, NB * s + j + 1)
                dve.scalar_tensor_tensor(kf[:, j], pa[job[0]][0:NP, 0:C], 1.0 / WS, bkb[0:NP, 0:C], ALU.mult, ALU.add)
                dve.scalar_tensor_tensor(vtl[:, j, 0:C], pa[job[0]][0:NP, C:2 * C], 1.0 / WS, vth[:, j, 0:C],
                                         ALU.mult, ALU.subtract).then_inc(a_free[job[0]], 1)
                if j == NB - 1:
                    dve.wait_ge(a_free[job[0]], job[1] + 1)

            def keys(s):
                dve.tensor_scalar(kf[:, :, :], kf[:, :, :], 0.0, EPS, ALU.max, ALU.add).then_inc(kf_ok, 1)

            def keys_scale(s):
                dve.wait_ge(kn_ok, s + 1)
                step(dve.tensor_scalar(kr[:, :], kn[:, :], 1e-12, 1.0 / KS, ALU.max, ALU.mult))
                step(dve.reciprocal(kr[:, :], kr[:, :]))
                dve.tensor_tensor(kf[:, :, :], kf[:, :, :], kr[:, :].unsqueeze(2).to_broadcast([NP, NB, C]),
                                  ALU.mult).then_inc(kx_ok, 1)

            def keys_low(s):
                dve.wait_ge(kh_ok, s + 1)
                dve.tensor_tensor(kl[:, :, :], kf[:, :, :], kh[:, :, :], ALU.subtract).then_inc(kl_ok, 1)

            def product(s):
                for c in range(CC):
                    job = A(s, VK + c)
                    full(dve, a_full, job)
                    bank = pa[job[0]]
                    step(dve.tensor_copy(km[:, c:c + 1], bank[:, C:C + 1]))
                    dve.scalar_tensor_tensor(vk[:, c], bkb[:, C:2 * C], km[:, c:c + 1], bank[:, 0:C],
                                             ALU.mult, ALU.add).then_inc(vk_ok, 1)
                    dve.wait_ge(vk_ok, CC * s + c + 1)
                    dve.nop().then_inc(a_free[job[0]], 1)

            def product_low(s):
                for c in range(CC):
                    dve.wait_ge(vkh_ok, CC * s + c + 1)
                    dve.scalar_tensor_tensor(vkl[:, c], vk[:, c], 1.0 / (KS * N), vkh[:, c],
                                             ALU.mult, ALU.subtract).then_inc(vkl_ok, 1)

            def query_low(s):
                dve.wait_ge(th_ok, s + 1)
                dve.tensor_tensor(tl[:, :, :], tf[:, :, :], th[:, :, :], ALU.subtract).then_inc(tl_ok, 1)

            def taps(s, par, c, first, n):
                if first == 0:
                    for h in range(2):
                        job = D(s, (0, 1, 4, 5)[2 * c + h])
                        full(dve, d_full, job)
                        dy, dx = divmod(KP, 5)
                        dve.scalar_tensor_tensor(
                            acc[:, c, h * HALF:(h + 1) * HALF].rearrange("p (a b) -> p a b", a=HR),
                            vp[:, par, c, h * HR + dy:h * HR + dy + HR, dx:dx + IMG], dw[:, c, KP:KP + 1],
                            pd[job[0]][:, 0:HALF].rearrange("p (a b) -> p a b", a=HR),
                            ALU.mult, ALU.add).then_inc(d_free[job[0]], 1)
                        dve.wait_ge(d_free[job[0]], job[1] + 1)
                    first, n = 1, n - 1
                whole = acc[:, c].rearrange("p (a b) -> p a b", a=IMG)
                for k in range(KP + first, min(KP + first + n, TAPS)):
                    dy, dx = divmod(k, 5)
                    step(dve.scalar_tensor_tensor(whole, vp[:, par, c, dy:dy + IMG, dx:dx + IMG], dw[:, c, k:k + 1],
                                                  whole, ALU.mult, ALU.add))

            def scaled(r):
                for h in range(2):
                    job = BJ(r, h)
                    full(dve, b_full, job)
                    for c in range(CC):
                        part = af[:, c, h * HALF:(h + 1) * HALF]
                        last = dve.scalar_tensor_tensor(part, part, col[:, 8 + c:9 + c], pb[job[0]][:, 0:HALF],
                                                        ALU.mult, ALU.mult)
                    last.then_inc(b_free[job[0]], 1)
                dve.wait_ge(b_free[1], BJ(r, 1)[1] + 1)
                dve.scalar_tensor_tensor(acc[:, :, :].rearrange("p c n -> p (c n)"),
                                         acc[:, :, :].rearrange("p c n -> p (c n)"), 1.0 / WS,
                                         af[:, :, :].rearrange("p c n -> p (c n)"), ALU.mult, ALU.add).then_inc(y_ok, 1)

            def y_low(r):
                dve.wait_ge(yh_ok, r + 1)
                dve.tensor_tensor(yl[:, :, :], acc[:, :, :], yh[:, :, :], ALU.subtract).then_inc(yl_ok, 1)

            def scale(s):
                full(dve, a_full, A(s, KZ))
                dve.wait_ge(a_free[SS % 4], A(s, SS)[1] + 1)
                step(dve.tensor_scalar(nn[:, :], nn[:, :], 1e-12, EPS, ALU.max, ALU.mult))
                dve.tensor_tensor(ww[:, :], nn[:, :], pa[KZ % 4][:, 0:Q], ALU.add).then_inc(a_free[KZ % 4], 1)
                dve.wait_ge(a_free[KZ % 4], A(s, KZ)[1] + 1)
                step(dve.scalar_tensor_tensor(nn[:, :], ww[:, :], EPS, ww[:, :], ALU.mult, ALU.mult))

            def scale_end(s):
                full(dve, a_full, A(s, A2))
                dve.tensor_tensor(ww[:, :], nn[:, :], pa[A2 % 4][:, 0:Q], ALU.add).then_inc(a_free[A2 % 4], 1)
                dve.wait_ge(a_free[A2 % 4], A(s, A2)[1] + 1)
                dve.nop().then_inc(ww_ok, 1)
                dve.wait_ge(fs_ok, s + 1)
                dve.reciprocal(sf[:, :], ww[:, :]).then_inc(sf_ok, 1)

            dve.memset(vp[:, :, :, :, :], 0.0).then_inc(pad_ok, 1)
            dve.memset(vh[:, :, :, :], 0.0)
            dve.memset(vl[:, :, :, :], 0.0).then_inc(pad_ok, 1)
            dve.memset(vth[:, :, C:C + 2], 1.0).then_inc(pad_ok, 1)
            dve.memset(vtl[:, :, C:C + 2], 0.0).then_inc(pad_ok, 1)
            dve.wait_ge(w_in, 64)
            step(dve.tensor_scalar(dw[:, :, :], dr[:, :, :], WS, None, ALU.mult))
            dve.wait_ge(w_hi, 1)
            dve.scalar_tensor_tensor(wl[:, :, :].rearrange("p c n -> p (c n)"), wf[:, :, :].rearrange("p c n -> p (c n)"), WS,
                                     wh[:, :, :].rearrange("p c n -> p (c n)"), ALU.mult, ALU.subtract).then_inc(w_ok, 1)
            for c in range(CC):
                for k in range(KP):
                    step(dve.tensor_scalar(dgf[:, :], idn, dw[:, c, k:k + 1], None, ALU.mult))
                    step(dve.tensor_copy(dgh[:, c, k], dgf[:, :]))
                    step(dve.tensor_tensor(dgl[:, c, k], dgf[:, :], dgh[:, c, k], ALU.subtract))
            dve.wait_ge(pb_ok, 1)
            for c in range(CC):
                dve.tensor_tensor(pbc[:, c:c + 1], pb[c][:, 0:1], col[:, 12 + c:13 + c], ALU.add).then_inc(dw_ok, 1)
            moments(0, 0, 0)
            statistics(0)

            def slot(s, par, half, kind):
                live, before = kind != "rest", kind != "first"
                r, rp = s - 1, 1 - par
                if live:
                    for j in range(NB):
                        pixels(s, j)
                        if before:
                            taps(r, rp, 1, 2 * j, 2)
                    keys(s)
                elif before:
                    taps(r, rp, 1, 0, TAPS)
                if before:
                    scaled(r)
                if live:
                    keys_scale(s)
                    keys_low(s)
                    query_low(s)
                if before:
                    y_low(r)
                if kind in ("first", ""):
                    moments(s + 1, 1 - par, half + 1 if par else half)
                if live:
                    product(s)
                    product_low(s)
                    taps(s, par, 0, 0, 4)
                if kind in ("first", ""):
                    statistics(s + 1)
                if live:
                    scale(s)
                    taps(s, par, 0, 4, TAPS)
                    scale_end(s)

            slot(0, 0, 0, "first")
            slot(1, 1, 0, "")
            slot(2, 0, 1, "")
            with dve.Fori(1, B // 2 - 1) as t:
                chain.loop(t - 1, DV_LOOP)
                slot(2 * t + 1, 1, t, "")
                slot(2 * t + 2, 0, t + 1, "")
            chain.end(B // 2 - 2)
            slot(B - 1, 1, B // 2 - 1, "last")
            slot(B, 0, B // 2, "rest")

        @block.tensor
        def _(pe):
            def products(bank, terms, sync=None):
                for n, (w, m) in enumerate(terms):
                    last = pe.matmul(bank, w, m, start=(n == 0), stop=(n == len(terms) - 1))
                if sync is not None:
                    last.then_inc(sync, 1)

            def pairs(hi_w, lo_w, hi_m, lo_m):
                return ((hi_w, hi_m), (hi_w, lo_m), (lo_w, hi_m))

            def keys_values(s, par):
                pe.wait_ge(hl_ok, s + 1)
                for j in range(NB):
                    job = A(s, KV + j)
                    free(pe, a_free, job)
                    px = slice(NP * j, NP * j + NP)
                    products(pa[job[0]][0:NP, :], [t for c in range(CC) for t in pairs(
                        hh[:, par, c, px], hl[:, par, c, px], wh[:, c, C:3 * C], wl[:, c, C:3 * C])], a_full[job[0]])

            def channels(s, par, first, w0):
                for m in range(CC):
                    for h in range(2):
                        job = A(s, first + 2 * m + h)
                        free(pe, a_free, job)
                        px, wc = slice(HALF * h, HALF * h + HALF), slice(w0 + P * m, w0 + P * m + P)
                        products(pa[job[0]][:, 0:HALF], [t for c in range(CC) for t in pairs(
                            wh[:, c, wc], wl[:, c, wc], hh[:, par, c, px], hl[:, par, c, px])], a_full[job[0]])

            def product(s):
                pe.wait_ge(kl_ok, s + 1)
                for c in range(CC):
                    job = A(s, VK + c)
                    free(pe, a_free, job)
                    ch = slice(P * c, P * c + P)
                    products(pa[job[0]][:, 0:C + 1], [t for j in range(NB) for t in pairs(
                        kh[:, j, ch], kl[:, j, ch], vth[:, j, 0:C + 1], vtl[:, j, 0:C + 1])], a_full[job[0]])

            def quarters(s, off, weight, moving):
                job = A(s, off)
                free(pe, a_free, job)
                for q in range(4):
                    for c in range(CC):
                        last = pe.matmul(pa[job[0]][32 * q:32 * q + 32, 0:Q], weight(c), moving[:, c, Q * q:Q * q + Q],
                                         start=(c == 0), stop=(c == CC - 1))
                last.then_inc(a_full[job[0]], 1)

            def attention(s):
                for m in range(CC):
                    for h in range(2):
                        job = A(s, AT + 2 * m + h)
                        free(pe, a_free, job)
                        px, ch = slice(HALF * h, HALF * h + HALF), slice(P * m, P * m + P)
                        products(pa[job[0]][:, 0:HALF], [t for c in range(CC) for t in pairs(
                            vkh[:, c, ch], vkl[:, c, ch], th[:, c, px], tl[:, c, px])], a_full[job[0]])

            def depthwise(s, c, h):
                job = D(s, (0, 1, 4, 5)[2 * c + h])
                free(pe, d_free, job)
                win = lambda v, k: v[:, c, h * HR + k // 5:h * HR + k // 5 + HR, k % 5:k % 5 + IMG]
                products(pd[job[0]][:, 0:HALF], [t for k in range(KP) for t in pairs(
                    dgh[:, c, k], dgl[:, c, k], win(vh, k), win(vl, k))], d_full[job[0]])

            def statistics(s):
                pe.wait_ge(rn_ok, s + 1)
                for c in range(CC):
                    job = stat_job(s, c)
                    free(pe, d_free, job)
                    products(pd[job[0]][:, 0:2], [(gavg, mv[:, c])], d_full[job[0]])

            def spread(r):
                pe.wait_ge(sf_ok, r + 1)
                for h in range(2):
                    job = BJ(r, h)
                    free(pe, b_free, job)
                    for k in range(2):
                        last = pe.matmul(pb[job[0]][:, Q * k:Q * k + Q], sl[:, 2 * h + k], sf[:, :],
                                         start=(k == 0), stop=True, skip_group_check=True)
                    last.then_inc(b_full[job[0]], 1)

            def project(r):
                pe.wait_ge(yl_ok, r + 1)
                for m in range(CC):
                    for h in range(2):
                        job = BJ(r, 2 + 2 * m + h)
                        free(pe, b_free, job)
                        px, wc = slice(HALF * h, HALF * h + HALF), slice(3 * C + P * m, 3 * C + P * m + P)
                        products(pb[job[0]][:, 0:HALF], [t for c in range(CC) for t in pairs(
                            wh[:, c, wc], wl[:, c, wc], yh[:, c, px], yl[:, c, px])], b_full[job[0]])

            pe.wait_ge(w_in, 64)
            for m in range(CC):
                products(pb[m][:, 0:1], [(wf[:, c, 3 * C + P * m:3 * C + P * m + P], col[:, 10 + c:11 + c])
                                         for c in range(CC)], pb_ok if m else None)
            statistics(0)
            pe.wait_ge(w_ok, 1)
            pe.wait_ge(dw_ok, 2)

            def slot(s, par, half, kind):
                live, before = kind != "rest", kind != "first"
                if live:
                    keys_values(s, par)
                    channels(s, par, V, 2 * C)
                    channels(s, par, QJ, 0)
                if before:
                    spread(s - 1)
                if live:
                    pe.wait_ge(vl_ok, CC * s + CC)
                    depthwise(s, 0, 0)
                    depthwise(s, 0, 1)
                    product(s)
                if before:
                    project(s - 1)
                if kind in ("first", ""):
                    statistics(s + 1)
                if live:
                    pe.wait_ge(tsq_ok, s + 1)
                    quarters(s, SS, lambda c: ones, sq)
                    pe.wait_ge(kmb_ok, CC * s + CC)
                    quarters(s, KZ, lambda c: kmb[:, c], tf)
                    pe.wait_ge(tl_ok, s + 1)
                    pe.wait_ge(vkl_ok, CC * s + CC)
                    attention(s)
                    depthwise(s, 1, 0)
                    pe.wait_ge(asq_ok, s + 1)
                    quarters(s, A2, lambda c: mean_ch, sq)
                    depthwise(s, 1, 1)

            slots(pe, slot)


_VECTORS = ["L0_conv_bias", "L1_conv_qkv_b", "L1_conv_qkv_b", "L1_conv_norm_w", "L1_conv_dwc_b", "L1_conv_proj_b"]
_FIRST = [0, 0, 2 * C, 0, 0, 0]


def _constants(np):
    group = np.kron(np.eye(P // GN), np.full((GN, GN), 1.0 / GN)).astype(np.float32)
    mask = np.tile(np.eye(JB) * GSC, (NE, 1)).astype(np.float32)
    l1c = np.zeros((P, 6 * P), np.float32)
    for q in range(4):
        l1c[32 * q, q * P:(q + 1) * P] = 1.0
    l1c[:, 4 * P:5 * P] = np.eye(P)
    for k, v in enumerate((1.0, 1.0 / C, 1.0 / (KS * N))):
        l1c[:, 5 * P + 32 * k:5 * P + 32 * k + 32] = v
    return group, mask, l1c


def kernel(**inputs):
    import numpy as np
    import concourse.bacc as bacc
    from concourse.bass_utils import run_bass_kernel_spmd

    a = {k: np.asarray(v) for k, v in inputs.items()}
    group, mask, l1c = _constants(np)
    rw = a["L0_conv_route_w"].reshape(NE, CC, P).transpose(2, 1, 0)
    route = np.concatenate([np.repeat(rw, JB, axis=2).reshape(P, CC * P), mask], axis=1)
    wmix = a["L0_conv_weight"].reshape(2, P // JB, JB, CC, P, 9, NE).transpose(0, 3, 5, 6, 2, 1, 4).reshape(2 * U, P, P * P // JB)
    cols = [np.full((P, 1), EPS, np.float32), np.repeat(a["L0_conv_route_b"], JB).reshape(P, 1)]
    for name, first in zip(_VECTORS, _FIRST):
        cols.append(a[name][first:first + C].reshape(CC, P).T)
    lw = np.concatenate([a["L1_conv_qkv_w"], a["L1_conv_proj_w"]], axis=0).T.reshape(CC, P, 4 * C).transpose(1, 0, 2)
    data = {
        "x": a["x"], "route": route, "wmix": wmix, "consts": group, "cols": np.concatenate(cols, axis=1), "lw": lw,
        "rows": np.broadcast_to(a["L1_conv_qkv_b"][C:3 * C], (P, 2 * C)), "l1c": l1c,
        "dwc": a["L1_conv_dwc_w"].reshape(CC, P, TAPS).transpose(1, 0, 2),
    }
    nc = bacc.Bacc("TRN2", target_bir_lowering=False, num_devices=1)
    data = {k: np.ascontiguousarray(v) for k, v in data.items()}
    args = {k: nc.dram_tensor(f"in_{k}", v.shape, F32, kind="ExternalInput").ap() for k, v in data.items()}
    wpair = nc.dram_tensor("wpair", (2 * U, P, 2 * P * P // JB), F16).ap()
    x1s = nc.dram_tensor("x1s", (B, CC, P, N), F32).ap()
    out = nc.dram_tensor("out", (B, C, IMG, IMG), F32, kind="ExternalOutput").ap()
    mk_conv_preact(nc, wpair=wpair, x1s=x1s, out=out, **args)
    r = run_bass_kernel_spmd(nc, [{f"in_{k}": v for k, v in data.items()}], core_ids=[0])
    return r.results[0]["out"]
```

```python
import concourse.bass as bass
from concourse import mybir
from contextlib import ExitStack

F32 = mybir.dt.float32
F32R = mybir.dt.float32r
F16 = mybir.dt.float16
ALU = mybir.AluOpType
ACT = mybir.ActivationFunctionType
AX = mybir.AxisListType

P = 128
B, C, IMG = 32, 256, 28
CC = C // P
N = IMG * IMG
HALF = N // 2
HR = IMG // 2
NE = 8
JB = P // NE
GS = 4
NG = B // GS
U = CC * 9
GN = 8
EPS = 1e-5
WS = 1024.0
GSC = 16.0
PAD1 = IMG + 2
KCH = [5, 4, 5, 4]
BANKS = 4
WR = 6
XR = 4
TAPS = 25
KP = 10
NB = 7
NP = N // NB
Q = N // 4
KS = 64.0
PAD2 = IMG + 4
VT = CC * (TAPS - KP)
EARLY = 12
LEAD = 4
TAP_ORDER = [(k, 0) for k in range(KP, KP + LEAD)] + [
    (k + LEAD * (c ^ 1), c) for k in range(KP, TAPS) for c in (1, 0) if k + LEAD * (c ^ 1) < TAPS]
DV_LOOP = 2 * (VT + 12)


class Tally:

    def __init__(self, sem):
        self.sem, self.total, self.local, self.i, self.per = sem, 0, 0, None, 0

    def loop(self, i, per):
        self.i, self.per, self.local = i, per, 0

    def end(self, turns):
        assert self.local == self.per, (self.local, self.per)
        self.total += self.per * turns
        self.i = None

    def inc(self, ins, n=1):
        ins.then_inc(self.sem, n)
        if self.i is None:
            self.total += n
        else:
            self.local += n

    def value(self):
        return self.total if self.i is None else self.i * self.per + (self.total + self.local)


def need(eng, sem, value):
    if isinstance(value, int) and value <= 0:
        return
    eng.wait_ge(sem, value)


def mk_conv_preact(nc, x, route, wmix, consts, cols, lw, rows, l1c, dwc, wpair, x1s, out):
    xv = x.rearrange("b (c p) h w -> b p c (h w)", c=CC)
    with ExitStack() as outer:
        def keep(kind, name, shape, dt=None):
            if kind == "sem":
                return outer.enter_context(nc.semaphore(name))
            return outer.enter_context(nc.sbuf_tensor(name, shape, dt))

        cst = keep("sb", "cst", [P, P], F32)
        col = keep("sb", "col", [P, cols.shape[1]], F32)
        rs = keep("sb", "rs", [P, B * CC], F32)
        nb = keep("sb", "nb", [P, B * CC], F32)
        bdh = keep("sb", "bdh", [P, B * JB], F16)
        bdl = keep("sb", "bdl", [P, B * JB], F16)
        gavg = cst[:, 0:P]
        eps = col[:, 0:1]

        prologue(nc, xv, route, wmix, consts, cols, wpair, cst, col, gavg, eps, rs, nb, bdh, bdl)
        routed_conv(nc, xv, wpair, x1s, col, rs, nb, bdh, bdl)
        if out is not None:
            linear_attention(nc, x1s, out, lw, rows, l1c, cst, col, dwc)


def prologue(nc, xv, route, wmix, consts, cols, wpair, cst, col, gavg, eps, rs, nb, bdh, bdl):
    NCH = 2 * U
    with ExitStack() as ctx:
        sb = lambda n, s, d: ctx.enter_context(nc.sbuf_tensor(n, s, d))
        sem = lambda n: ctx.enter_context(nc.semaphore(n))
        WB = 3
        wf = sb("wf", [P, WB, 1024], F32)
        wp = sb("wp", [P, WB, 2, 1024], F16)
        xs = sb("xs", [P, XR, CC, N], F32)
        bn = sb("bn", [P, XR, CC, 2, 6], F32)
        mv = sb("mv", [P, B * CC, 2], F32)
        mt = sb("mt", [P, B * CC, 2], F32)
        tmp = sb("tmp", [P, B * CC], F32)
        tm2 = sb("tm2", [P, B * CC], F32)
        std = sb("std", [P, B * CC], F32)
        se = sb("se", [P, B, CC], F32)
        rw = sb("rw", [P, CC, P], F32)
        gate = sb("gate", [P, B], F32)
        hb = sb("hb", [P, 1], F32)
        mask = sb("mask", [P, JB], F32)
        bdf = sb("bdf", [P, B, JB], F32)
        pstat = ctx.enter_context(nc.psum_tensor("pstat", [P, 512], F32))
        pgate = ctx.enter_context(nc.psum_tensor("pgate", [P, 512], F32))
        small_in = sem("small_in")
        w_in = [sem(f"w_in{i}") for i in range(WB)]
        w_out = [sem(f"w_out{i}") for i in range(WB)]
        x_in = [sem(f"x_in{i}") for i in range(XR)]
        w_hi, w_lo = sem("w_hi"), sem("w_lo")
        stats = sem("stats")
        stat_pe, gate_pe, std_ok, gate_ok, v_step = sem("stat_pe"), sem("gate_pe"), sem("std_ok"), sem("gate_ok"), sem("v_step")
        block = ctx.enter_context(nc.Block())

        @block.sync
        def _(sp):
            sp.dma_start(cst[:, :], consts).then_inc(small_in, 16)
            sp.dma_start(col[:, :], cols).then_inc(small_in, 16)
            sp.dma_start(rw[:, :, :], route[:, 0:CC * P].rearrange("p (c m) -> p c m", c=CC)).then_inc(small_in, 16)
            sp.dma_start(mask[:, :], route[:, CC * P:CC * P + JB]).then_inc(small_in, 16)
            for n in range(max(NCH, B)):
                if n < B:
                    need(sp, stats, n - XR + 1)
                    sp.dma_start(xs[:, n % XR], xv[n]).then_inc(x_in[n % XR], 16)
                need(sp, w_lo, n - WB + 1)
                sp.dma_start(wf[:, n % WB], wmix[n]).then_inc(w_in[n % WB], 16)

        @block.gpsimd
        def _(pool):
            for n in range(NCH):
                pool.wait_ge(w_lo, n + 1)
                pool.dma_start(wpair[n], wp[:, n % WB].rearrange("p k f -> p (k f)")).then_inc(w_out[n % WB], 16)
            for k in range(WB):
                pool.wait_ge(w_out[k], 16 * len(range(k, NCH, WB)))

        @block.scalar
        def _(act):
            for n in range(NCH):
                act.wait_ge(w_in[n % WB], 16 * (n // WB + 1))
                if n >= WB:
                    act.wait_ge(w_out[n % WB], 16 * (n // WB))
                act.activation(wp[:, n % WB, 0], wf[:, n % WB], ACT.Copy, scale=WS).then_inc(w_hi, 1)
            act.wait_ge(small_in, 64)
            act.wait_ge(v_step, 5)
            act.activation(std[:, :], tmp[:, :], ACT.Sqrt).then_inc(std_ok, 1)
            act.wait_ge(gate_pe, 1)
            act.wait_ge(v_step, 13)
            act.activation(gate[:, :], pgate[:, 0:B], ACT.Tanh, scale=0.5, bias=hb[:, :]).then_inc(gate_ok, 1)

        @block.vector
        def _(dve):
            steps = Tally(v_step)

            def step(ins):
                steps.inc(ins)
                dve.wait_ge(v_step, steps.value())

            for n in range(max(NCH, B)):
                if n < B:
                    k = n % XR
                    dve.wait_ge(x_in[k], 16 * (n // XR + 1))
                    for c in range(CC):
                        for h in range(2):
                            last = dve.bn_stats(bn[:, k, c, h], xs[:, k, c, h * HALF:(h + 1) * HALF])
                    last.then_inc(stats, 1)
                dve.wait_ge(w_hi, n + 1)
                dve.scalar_tensor_tensor(wp[:, n % WB, 1], wf[:, n % WB], WS, wp[:, n % WB, 0],
                                         ALU.mult, ALU.subtract).then_inc(w_lo, 1)
                if n < B:
                    dve.wait_ge(stats, n + 1)
                    for c in range(CC):
                        last = dve.bn_aggr(mv[:, n * CC + c], bn[:, k, c])
            mean, sq = mv[:, :, 0], mv[:, :, 1]
            step(last)
            step(dve.tensor_tensor(tmp[:, :], mean, mean, ALU.mult))
            step(dve.tensor_tensor(sq, sq, tmp[:, :], ALU.add))
            dve.wait_ge(stat_pe, 1)
            step(dve.tensor_copy(mt[:, :, :], pstat[:, 0:2 * B * CC].rearrange("p (a b) -> p a b", b=2)))
            dve.tensor_tensor(tm2[:, :], mt[:, :, 0], mt[:, :, 0], ALU.mult).then_inc(stats, 1)
            dve.wait_ge(stats, B + 1)
            dve.tensor_tensor(tmp[:, :], mt[:, :, 1], tm2[:, :], ALU.subtract).then_inc(stats, 1)
            dve.wait_ge(stats, B + 2)
            step(dve.tensor_scalar(tmp[:, :], tmp[:, :], 0.0, EPS, ALU.max, ALU.add))
            dve.wait_ge(std_ok, 1)
            step(dve.reciprocal(rs[:, :], std[:, :]))
            step(dve.tensor_tensor(tm2[:, :], rs[:, :], rs[:, :], ALU.mult))
            step(dve.scalar_tensor_tensor(tm2[:, :], tmp[:, :], -0.5, tm2[:, :], ALU.mult, ALU.mult))
            step(dve.scalar_tensor_tensor(rs[:, :], tm2[:, :], 1.5, rs[:, :], ALU.add, ALU.mult))
            step(dve.scalar_tensor_tensor(nb[:, :], mt[:, :, 0], -1.0, rs[:, :], ALU.mult, ALU.mult))
            step(dve.tensor_tensor(tm2[:, :], mean, rs[:, :], ALU.mult))
            step(dve.tensor_tensor(se[:, :, :].rearrange("p b c -> p (b c)"), tm2[:, :], nb[:, :], ALU.add))
            step(dve.tensor_scalar(hb[:, :], col[:, 1:2], 0.5, None, ALU.mult))
            dve.wait_ge(gate_ok, 1)
            step(dve.tensor_scalar(gate[:, :], gate[:, :], 0.5, 0.5, ALU.mult, ALU.add))
            step(dve.tensor_tensor(bdf[:, :, :], gate[:, :].unsqueeze(2).to_broadcast([P, B, JB]),
                                   mask[:, :].unsqueeze(1).to_broadcast([P, B, JB]), ALU.mult))
            bd = bdf[:, :, :].rearrange("p b j -> p (b j)")
            step(dve.tensor_copy(bdh[:, :], bd))
            step(dve.tensor_tensor(bdl[:, :], bd, bdh[:, :], ALU.subtract))

        @block.tensor
        def _(pe):
            pe.wait_ge(small_in, 64)
            pe.wait_ge(v_step, 3)
            pe.matmul(pstat[:, 0:2 * B * CC], gavg, mv[:, :, :].rearrange("p a b -> p (a b)"),
                      start=True, stop=True).then_inc(stat_pe, 1)
            pe.wait_ge(v_step, 12)
            for c in range(CC):
                last = pe.matmul(pgate[:, 0:B], rw[:, c], se[:, :, c], start=(c == 0), stop=(c == CC - 1))
            last.then_inc(gate_pe, 1)


def routed_conv(nc, xv, wpair, x1s, col, rs, nb, bdh, bdl):
    with ExitStack() as ctx:
        sb = lambda n, s, d: ctx.enter_context(nc.sbuf_tensor(n, s, d))
        sem = lambda n: ctx.enter_context(nc.semaphore(n))
        wdh = sb("wdh", [P, 2, GS, U, P], F16)
        wdl = sb("wdl", [P, 2, GS, U, P], F16)
        wr = sb("wr", [P, WR, 2, 1024], F16)
        xg = sb("xg", [P, GS, CC, N], F32)
        xh = sb("xh", [P, GS, CC, PAD1, PAD1], F16)
        xl = sb("xl", [P, GS, CC, PAD1, PAD1], F16)
        xf = sb("xf", [P, CC, N], F32)
        bg = sb("bg", [P, 2, GS * JB], F16)
        pm = [ctx.enter_context(nc.psum_tensor(f"pm{k}", [P, 512], F32)) for k in range(4)]
        pc = [ctx.enter_context(nc.psum_tensor(f"pc{k}", [P, 512], F32)) for k in range(4)]
        w_in = [sem(f"wr_in{k}") for k in range(WR)]
        x_in = [sem(f"xg_in{k}") for k in range(GS)]
        x1_out = [sem(f"x1_out{k}") for k in range(GS)]
        mixed, mix_hi, mix_lo = sem("mixed"), sem("mix_hi"), sem("mix_lo")
        conv_done, conv_out = sem("conv_done"), sem("conv_out")
        bg_ok, xf_ok, xh_ok, xl_ok, xb_ok = sem("bg_ok"), sem("xf_ok"), sem("xh_ok"), sem("xl_ok"), sem("xb_ok")
        block = ctx.enter_context(nc.Block())

        def over_groups(eng, body):
            with eng.Fori(0, NG - 1) as g:
                body(g, False)
            body(NG - 1, True)

        def chunk(g, H, u):
            return 36 * g + 18 * H + u

        def job(g, H, i):
            return 16 * g + 8 * H + 2 * i

        def chunks(H, i):
            first = sum(KCH[:i])
            return range(first, first + KCH[i])

        @block.sync
        def _(sp):
            def load_w(g, H, u):
                n = chunk(g, H, u)
                need(sp, mixed, n - WR + 1)
                sp.dma_start(wr[:, u % WR].rearrange("p k f -> p (k f)"), wpair[U * H + u]).then_inc(w_in[u % WR], 16)

            def load_x(g, i):
                if not isinstance(g, int) or g:
                    sp.wait_ge(x1_out[i], 32 * g)
                s = GS * g + i
                src = xv[s] if isinstance(s, int) else xv[bass.ds(s, 1)].rearrange("a p c n -> (a p) c n")
                sp.dma_start(xg[:, i], src).then_inc(x_in[i], 16)

            def store(g, H, i):
                sp.wait_ge(conv_out, BANKS + job(g, H, i) + 2)
                s = GS * g + i
                dst = x1s[s, H] if isinstance(s, int) else x1s[bass.ds(s, 1), H].rearrange("a p n -> (a p) n")
                sp.dma_start(dst, xg[:, i, H]).then_inc(x1_out[i], 16)

            for i in range(GS):
                load_x(0, i)
            for u in range(U):
                load_w(0, 0, u)

            def body(g, last):
                for H in range(2):
                    for i in range(GS):
                        if not (last and H):
                            for u in chunks(H, i):
                                load_w(g + H, 1 - H, u)
                        if i:
                            store(g, H, i - 1)
                        if H and not last and i:
                            load_x(g + 1, i - 1)
                    store(g, H, GS - 1)
                if not last:
                    load_x(g + 1, GS - 1)

            over_groups(sp, body)
            for i in range(GS):
                sp.wait_ge(x1_out[i], 32 * NG)

        @block.gpsimd
        def _(pool):
            def low(g, i):
                s = GS * g + i
                for c in range(CC):
                    pool.wait_ge(xh_ok, 2 * s + c + 1)
                    pool.tensor_tensor(xl[:, i, c, 1:1 + IMG, 1:1 + IMG],
                                       xf[:, c].rearrange("p (a b) -> p a b", a=IMG),
                                       xh[:, i, c, 1:1 + IMG, 1:1 + IMG], ALU.subtract).then_inc(xl_ok, 1)

            for i in range(GS):
                low(0, i)

            def body(g, last):
                for H in range(2):
                    for i in range(GS):
                        if H and not last and i:
                            low(g + 1, i - 1)
                if not last:
                    low(g + 1, GS - 1)

            over_groups(pool, body)

        @block.scalar
        def _(act):
            def high(g, i):
                s = GS * g + i
                act.wait_ge(x_in[i], 16 * g + 16)
                if isinstance(g, int) and g == 0:
                    act.wait_ge(conv_out, BANKS)
                for c in range(CC):
                    need(act, xl_ok, 2 * s + c - 1)
                    k = CC * s + c
                    sc = rs[:, k:k + 1] if isinstance(k, int) else rs[:, bass.ds(k, 1)]
                    bi = nb[:, k:k + 1] if isinstance(k, int) else nb[:, bass.ds(k, 1)]
                    act.activation(xf[:, c], xg[:, i, c], ACT.Identity, scale=sc, bias=bi).then_inc(xf_ok, 1)
                for c in range(CC):
                    act.wait_ge(xf_ok, 2 * s + c + 1)
                    act.activation(xh[:, i, c, 1:1 + IMG, 1:1 + IMG],
                                   xf[:, c].rearrange("p (a b) -> p a b", a=IMG), ACT.Copy).then_inc(xh_ok, 1)
                for c in range(CC):
                    act.activation(xg[:, i, c], xg[:, i, c], ACT.Identity, bias=col[:, 2 + c:3 + c]).then_inc(xb_ok, 1)

            def mix(g, H, u):
                n = chunk(g, H, u)
                act.wait_ge(mixed, n + 1)
                act.activation(wdh[:, H, :, u, :], pm[(2 * H + u) % 4][:, :].rearrange("p (b m) -> p b m", b=GS),
                               ACT.Copy, scale=1.0 / GSC).then_inc(mix_hi, 1)

            def gates(g):
                if not (isinstance(g, int) and g == 0):
                    act.wait_ge(mixed, 36 * g)
                for k, src in enumerate((bdh, bdl)):
                    part = src[:, 0:GS * JB] if isinstance(g, int) and g == 0 else src[:, bass.ds(GS * JB * g, GS * JB)]
                    act.activation(bg[:, k], part, ACT.Copy).then_inc(bg_ok, 1)

            gates(0)
            high(0, 0)
            for u in range(U):
                mix(0, 0, u)
            for i in range(1, GS):
                high(0, i)

            def body(g, last):
                for H in range(2):
                    if H and not last:
                        gates(g + 1)
                    for i in range(GS):
                        if not (last and H):
                            for u in chunks(H, i):
                                mix(g + H, 1 - H, u)
                        if H and not last and i:
                            high(g + 1, i - 1)
                if not last:
                    high(g + 1, GS - 1)

            over_groups(act, body)

        @block.vector
        def _(dve):
            for tile in (xh, xl):
                for i in range(0, GS, 2):
                    dve.memset(tile[:, i:i + 2], 0.0).then_inc(conv_out, 1)

            def mix(g, H, u):
                n = chunk(g, H, u)
                dve.wait_ge(mix_hi, n + 1)
                dve.scalar_tensor_tensor(wdl[:, H, :, u, :], pm[(2 * H + u) % 4][:, :].rearrange("p (b m) -> p b m", b=GS),
                                         1.0 / GSC, wdh[:, H, :, u, :], ALU.mult, ALU.subtract).then_inc(mix_lo, 1)

            def add(g, H, i):
                if H == 0:
                    dve.wait_ge(xb_ok, 2 * (GS * g + i) + 2)
                for h in range(2):
                    dve.wait_ge(conv_done, job(g, H, i) + h + 1)
                    part = xg[:, i, H, h * HALF:(h + 1) * HALF]
                    dve.scalar_tensor_tensor(part, pc[(2 * i + h) % 4][:, 0:HALF], 1.0 / WS, part,
                                             ALU.mult, ALU.add).then_inc(conv_out, 1)

            for u in range(U):
                mix(0, 0, u)

            def body(g, last):
                for H in range(2):
                    for i in range(GS):
                        if not (last and H):
                            for u in chunks(H, i):
                                mix(g + H, 1 - H, u)
                        add(g, H, i)

            over_groups(dve, body)

        @block.tensor
        def _(pe):
            def mix(g, H, u):
                n = chunk(g, H, u)
                if u == 0 and H == 0:
                    pe.wait_ge(bg_ok, 2 * g + 2)
                pe.wait_ge(w_in[u % WR], 16 * (6 * g + 3 * H + u // WR + 1))
                need(pe, mix_lo, n - 3)
                bank = pm[(2 * H + u) % 4][:, :].rearrange("p (b m) -> p b m", b=GS)
                for jb in range(8):
                    dst = bank[:, :, jb * JB:(jb + 1) * JB]
                    for k, (wk, gk) in enumerate(((0, 0), (0, 1), (1, 0))):
                        last = pe.matmul(dst, wr[:, u % WR, wk, jb * P:(jb + 1) * P],
                                         bg[:, gk].rearrange("p (b j) -> p b j", b=GS),
                                         start=(k == 0 and jb == 0), stop=(k == 2), skip_group_check=True)
                last.then_inc(mixed, 1)

            def conv(g, H, i, after):
                pe.wait_ge(mix_lo, 36 * g + 18 * H + 18)
                pe.wait_ge(xl_ok, 2 * (GS * g + i) + 2)
                pe.wait_ge(conv_out, job(g, H, i) + BANKS - 2)
                for u in range(U):
                    c, t = divmod(u, 9)
                    dy, dx = divmod(t, 3)
                    for wk, xk in ((wdh, xh), (wdh, xl), (wdl, xh)):
                        for h in range(2):
                            q = pe.matmul(pc[(2 * i + h) % 4][:, 0:HALF], wk[:, H, i, u, :],
                                          xk[:, i, c, h * HR + dy:h * HR + dy + HR, dx:dx + IMG],
                                          start=(u == 0 and wk is wdh and xk is xh), stop=(u == U - 1 and wk is wdl))
                            if u == U - 1 and wk is wdl:
                                q.then_inc(conv_done, 1)
                    if u in after:
                        mix(*after[u])

            for u in range(U):
                mix(0, 0, u)

            def body(g, last):
                for H in range(2):
                    for i in range(GS):
                        after = {}
                        if not (last and H):
                            for k, u in enumerate(chunks(H, i)):
                                after[3 * k + 2] = (g + H, 1 - H, u)
                        conv(g, H, i, after)

            over_groups(pe, body)


def linear_attention(nc, x1s, out, lw, rows, l1c, cst, col, dwc):
    ov = out.rearrange("b (c p) h w -> b p c (h w)", c=CC)
    eps, gavg = col[:, 0:1], cst[:, 0:P]
    with ExitStack() as ctx:
        sb = lambda n, s, d=F32: ctx.enter_context(nc.sbuf_tensor(n, s, d))
        sem = lambda n: ctx.enter_context(nc.semaphore(n))
        wf = sb("wf1", [P, CC, 4 * C])
        wh = sb("wh", [P, CC, 4 * C], F16)
        wl = sb("wl", [P, CC, 4 * C], F16)
        bkb = sb("bkb", [P, 2 * C])
        kc = sb("kc", [P, 6 * P])
        dr = sb("dr", [P, CC, TAPS])
        dw = sb("dw", [P, CC, TAPS])
        dgf = sb("dgf", [P, P])
        dgh = sb("dgh", [P, CC, KP, P], F16)
        dgl = sb("dgl", [P, CC, KP, P], F16)
        pbc = sb("pbc", [P, CC])
        xb = sb("xb", [P, 2, CC, N])
        bn = sb("bn1", [P, CC, 2, 6])
        mv = sb("mv1", [P, CC, 2])
        mt = sb("mt1", [P, CC, 2])
        t1 = sb("t11", [P, CC])
        t2 = sb("t12", [P, CC])
        sd = sb("sd1", [P, CC])
        r1 = sb("r11", [P, CC])
        n1 = sb("n11", [P, CC])
        hf = sb("hf", [P, CC, N])
        hh = sb("hh", [P, 2, CC, N], F16)
        hl = sb("hl", [P, 2, CC, N], F16)
        kf = sb("kf", [NP, NB, C])
        ks = sb("ks", [NP, NB, C])
        kq = sb("kq", [NP, NB])
        kn = sb("kn", [NP, NB])
        kr = sb("kr", [NP, NB])
        kh = sb("kh", [NP, NB, C], F16)
        kl = sb("kl", [NP, NB, C], F16)
        vth = sb("vth", [NP, NB, C + 2], F16)
        vtl = sb("vtl", [NP, NB, C + 2], F16)
        vk = sb("vk", [P, CC, C])
        vkh = sb("vkh", [P, CC, C], F32R)
        vkl = sb("vkl", [P, CC, C], F32R)
        km = sb("km", [P, CC])
        kmb = sb("kmb", [P, CC, 32])
        tf = sb("tf", [P, CC, N])
        th = sb("th", [P, CC, N], F32R)
        tl = sb("tl", [P, CC, N], F32R)
        sq = sb("sq", [P, CC, N])
        af = sb("af", [P, CC, N])
        nn = sb("nn", [P, Q])
        ww = sb("ww", [P, Q])
        sf = sb("sf", [P, Q])
        vp = sb("vp", [P, 2, CC, PAD2, PAD2])
        vh = sb("vh", [P, CC, PAD2, PAD2], F16)
        vl = sb("vl", [P, CC, PAD2, PAD2], F16)
        acc = sb("acc", [P, 2, CC, N])
        yh = sb("yh", [P, CC, N], F16)
        yl = sb("yl", [P, CC, N], F16)
        of = sb("of", [P, CC, N])
        xr = sb("xr", [P, 2, CC, N])

        sl = kc[:, 0:4 * P].rearrange("p (q m) -> p q m", q=4)
        idn = kc[:, 4 * P:5 * P]
        ones, mean_ch, mean_px = kc[:, 5 * P:5 * P + 32], kc[:, 5 * P + 32:5 * P + 64], kc[:, 5 * P + 64:5 * P + 96]
        psum = lambda n: ctx.enter_context(nc.psum_tensor(n, [P, 512], F32))
        pa, pd, pb = [psum(f"pa{k}") for k in range(4)], [psum(f"pd{k}") for k in range(2)], [psum(f"pb{k}") for k in range(2)]
        a_full, a_free = [sem(f"a_full{k}") for k in range(4)], [sem(f"a_free{k}") for k in range(4)]
        d_full, d_free = [sem(f"d_full{k}") for k in range(2)], [sem(f"d_free{k}") for k in range(2)]
        b_full, b_free = [sem(f"b_full{k}") for k in range(2)], [sem(f"b_free{k}") for k in range(2)]
        w_in, w_hi, w_ok, pad_ok, dw_ok, dg_f, dg_h, pb_ok = [sem("l1_" + n) for n in (
            "w_in", "w_hi", "w_ok", "pad_ok", "dw_ok", "dg_f", "dg_h", "pb_ok")]
        xb_in, xr_in, o_out = [[sem(f"{n}{k}") for k in range(2)] for n in ("xb_in", "xr_in", "o_out")]
        bn_ok, mv_ok, sd_ok, rn_ok, hf_ok, hh_ok, hl_ok = [sem(n) for n in ("bn_ok", "mv_ok", "sd_ok", "rn_ok", "hf_ok", "hh_ok", "hl_ok")]
        vt_hi, kv_out, kf_ok, ksq_ok, kq_ok, kn_ok, kx_ok, kh_ok, kl_ok = [sem(n) for n in (
            "vt_hi", "kv_out", "kf_ok", "ksq_ok", "kq_ok", "kn_ok", "kx_ok", "kh_ok", "kl_ok")]
        vp_ok, vh_ok, vl_ok, dp_ok = [sem(n) for n in ("vp_ok", "vh_ok", "vl_ok", "dp_ok")]
        qr_ok, tf_ok, th_ok, tsq_ok, tl_ok = [sem(n) for n in ("qr_ok", "tf_ok", "th_ok", "tsq_ok", "tl_ok")]
        vk_ok, vkh_ok, kmb_ok, vkl_ok = [sem(n) for n in ("vk_ok", "vkh_ok", "kmb_ok", "vkl_ok")]
        af_ok, asq_ok, nn_ok, ww_ok, fs_ok, sf_ok = [sem(n) for n in ("af_ok", "asq_ok", "nn_ok", "ww_ok", "fs_ok", "sf_ok")]
        y_ok, yh_ok, yl_ok, of_ok, o_ok, dv = [sem(n) for n in ("y_ok", "yh_ok", "yl_ok", "of_ok", "o_ok", "dv")]
        block = ctx.enter_context(nc.Block())

        V, KV, QJ, VK, SS, KZ, AT, JOBS = 0, 4, 11, 15, 17, 18, 19, 23
        A = lambda s, off: (off % 4, (JOBS + 3 - off % 4) // 4 * s + off // 4)
        D = lambda s, off: (off % 2, (5 - off % 2 + 1) // 2 * s + off // 2)

        def BJ(r, off):
            return off % 2, 4 * r + 3 + off // 2 - (max(r - (B - 3), 0) if isinstance(r, int) else 0)

        def stat_job(s, c):
            return c, s if isinstance(s, int) and s < 2 else 4 * s - 6

        def full(eng, sems, job):
            eng.wait_ge(sems[job[0]], job[1] + 1)

        def free(eng, sems, job):
            need(eng, sems[job[0]], job[1])

        def slots(eng, slot, ahead=0):
            slot(0, 0, 0, "first")
            slot(1, 1, 0, "")
            slot(2, 0, 1, "")
            with eng.Fori(1, B // 2 - 1 - ahead) as t:
                slot(2 * t + 1, 1, t, "")
                slot(2 * t + 2, 0, t + 1, "")
            for t in range(B // 2 - 1 - ahead, B // 2 - 1):
                slot(2 * t + 1, 1, t, "")
                slot(2 * t + 2, 0, t + 1, "")
            slot(B - 1, 1, B // 2 - 1, "last")
            slot(B, 0, B // 2, "rest")

        def image(dram, s):
            if isinstance(s, int):
                return dram[s]
            return dram[bass.ds(s, 1)].rearrange("a p c n -> (a p) c n")

        x1v = x1s.rearrange("b c p n -> b p c n")

        @block.sync
        def _(sp):
            for dst, src in ((wf[:, :, :], lw), (bkb[:, :], rows), (kc[:, :], l1c), (dr[:, :, :], dwc)):
                sp.dma_start(dst, src).then_inc(w_in, 16)

            def load(s, par):
                if not (isinstance(s, int) and s < 2):
                    sp.wait_ge(hf_ok, s - 1)
                sp.dma_start(xb[:, par], image(x1v, s)).then_inc(xb_in[par], 16)

            def slot(s, par, half, kind):
                if not (isinstance(s, int) and s + 2 >= B):
                    load(s + 2, par)
                if kind != "first":
                    r, rp = s - 1, 1 - par
                    rh = half if par else half - 1
                    if not (isinstance(s, int) and s < 3):
                        need(sp, o_out[rp], 16 * rh)
                    sp.dma_start(xr[:, rp], image(x1v, r)).then_inc(xr_in[rp], 16)
                    sp.wait_ge(o_ok, CC * (r + 1))
                    sp.dma_start(image(ov, r), xr[:, rp]).then_inc(o_out[rp], 16)

            load(0, 0)
            load(1, 1)
            slots(sp, slot, 1)
            for k in range(2):
                sp.wait_ge(o_out[k], 16 * (B // 2))

        @block.gpsimd
        def _(pool):
            def norm_low(s, par):
                pool.wait_ge(hh_ok, s + 1)
                for c in range(CC):
                    last = pool.tensor_tensor(hl[:, par, c], hf[:, c], hh[:, par, c], ALU.subtract)
                last.then_inc(hl_ok, 1)

            def v_low(s, par):
                pool.wait_ge(vh_ok, s + 1)
                for c in range(CC):
                    pool.tensor_tensor(vl[:, c, 2:2 + IMG, 2:2 + IMG], vp[:, par, c, 2:2 + IMG, 2:2 + IMG],
                                       vh[:, c, 2:2 + IMG, 2:2 + IMG], ALU.subtract).then_inc(vl_ok, 1)

            def residual(r, rp, rh):
                pool.wait_ge(xr_in[rp], 16 * (rh + 1))
                for c in range(CC):
                    pool.wait_ge(of_ok, 4 * r + 2 * c + 2)
                    pool.tensor_tensor(xr[:, rp, c], xr[:, rp, c], of[:, c], ALU.add).then_inc(o_ok, 1)

            pool.wait_ge(pad_ok, 4)
            norm_low(0, 0)

            def slot(s, par, half, kind):
                if kind != "rest":
                    v_low(s, par)
                if kind in ("first", ""):
                    norm_low(s + 1, 1 - par)
                if kind != "first":
                    residual(s - 1, 1 - par, half if par else half - 1)

            slots(pool, slot)

        @block.scalar
        def _(act):
            def norm_root(s):
                act.wait_ge(mv_ok, 2 * s + 1)
                act.activation(sd[:, :], sd[:, :], ACT.Sqrt, bias=eps).then_inc(sd_ok, 1)

            def norm(s, par):
                act.wait_ge(mv_ok, 2 * s + 2)
                need(act, hl_ok, s)
                for c in range(CC):
                    last = act.activation(hf[:, c], xb[:, par, c], ACT.Identity, scale=r1[:, c:c + 1], bias=n1[:, c:c + 1])
                last.then_inc(hf_ok, 1)

            def norm_high(s, par):
                act.wait_ge(hf_ok, s + 1)
                act.activation(hh[:, par], hf[:, :, :], ACT.Copy).then_inc(hh_ok, 1)

            def v_pixels(s, j):
                job = A(s, KV + j)
                full(act, a_full, job)
                act.activation(vth[:, j, 0:C], pa[job[0]][0:NP, C:2 * C], ACT.Copy, scale=1.0 / WS).then_inc(vt_hi, 1)

            def keys(s):
                act.wait_ge(kf_ok, s + 1)
                act.activation(kf[:, :, :], kf[:, :, :], ACT.Square).then_inc(ksq_ok, 1)
                act.wait_ge(ksq_ok, s + 1)
                for j in range(NB):
                    act.activation(ks[:, j], kf[:, j], ACT.Square, accum_out=kq[:, j:j + 1]).then_inc(kq_ok, 1)
                act.wait_ge(kq_ok, NB * s + NB)
                act.activation(kn[:, :], kq[:, :], ACT.Sqrt).then_inc(kn_ok, 1)

            def keys_high(s):
                act.wait_ge(kx_ok, s + 1)
                act.activation(kh[:, :, :], kf[:, :, :], ACT.Copy).then_inc(kh_ok, 1)

            def values(s, par, before):
                need(act, y_ok, s - 1)
                for c in range(CC):
                    for h in range(2):
                        job = A(s, V + 2 * c + h)
                        full(act, a_full, job)
                        act.activation(vp[:, par, c, 2 + h * HR:2 + h * HR + HR, 2:2 + IMG],
                                       pa[job[0]][:, 0:HALF].rearrange("p (a b) -> p a b", a=HR), ACT.Identity,
                                       scale=1.0 / WS, bias=col[:, 6 + c:7 + c]).then_inc(a_free[job[0]], 1)
                        act.wait_ge(a_free[job[0]], job[1] + 1)
                if not (isinstance(s, int) and s == 0):
                    full(act, d_full, D(s - 1, 3))
                if before:
                    scale(s - 1)
                for c in range(CC):
                    last = act.activation(vh[:, c, 2:2 + IMG, 2:2 + IMG], vp[:, par, c, 2:2 + IMG, 2:2 + IMG], ACT.Copy)
                last.then_inc(vh_ok, 1)

            def queries(s):
                for c in range(CC):
                    for h in range(2):
                        job = A(s, QJ + 2 * c + h)
                        full(act, a_full, job)
                        act.activation(tf[:, c, h * HALF:(h + 1) * HALF], pa[job[0]][:, 0:HALF], ACT.Relu,
                                       scale=1.0 / WS, bias=col[:, 4 + c:5 + c]).then_inc(a_free[job[0]], 1)
                        act.wait_ge(a_free[job[0]], job[1] + 1)

            def queries_square(s):
                act.activation(tf[:, :, :], tf[:, :, :], ACT.Square, bias=eps).then_inc(tf_ok, 1)

            def queries_end(s):
                act.wait_ge(tf_ok, s + 1)
                act.activation(th[:, :, :], tf[:, :, :], ACT.Copy).then_inc(th_ok, 1)
                act.activation(sq[:, :, :], tf[:, :, :], ACT.Square).then_inc(tsq_ok, 1)

            def product_high(s):
                for c in range(CC):
                    act.wait_ge(vk_ok, CC * s + c + 1)
                    act.activation(vkh[:, c], vk[:, c], ACT.Copy, scale=1.0 / (KS * N)).then_inc(vkh_ok, 1)
                    act.activation(kmb[:, c], mean_px, ACT.Copy, scale=km[:, c:c + 1]).then_inc(kmb_ok, 1)

            def attention(s):
                full(act, a_full, A(s, SS))
                act.activation(nn[:, :], pa[SS % 4][:, 0:Q], ACT.Sqrt).then_inc(a_free[SS % 4], 1)
                need(act, y_ok, s)
                for c in range(CC):
                    for h in range(2):
                        job = A(s, AT + 2 * c + h)
                        full(act, a_full, job)
                        act.activation(af[:, c, h * HALF:(h + 1) * HALF], pa[job[0]][:, 0:HALF],
                                       ACT.Copy).then_inc(a_free[job[0]], 1)
                        act.wait_ge(a_free[job[0]], job[1] + 1)
                act.activation(sq[:, :, :], af[:, :, :], ACT.Square).then_inc(asq_ok, 1)

            def scale(s):
                act.wait_ge(ww_ok, s + 1)
                act.activation(ww[:, :], ww[:, :], ACT.Sqrt).then_inc(fs_ok, 1)

            def depthwise(s, par, c):
                for h in range(2):
                    job = D(s, 2 * c + h)
                    full(act, d_full, job)
                    act.activation(acc[:, par, c, h * HALF:(h + 1) * HALF], pd[job[0]][:, 0:HALF],
                                   ACT.Copy).then_inc(d_free[job[0]], 1)
                    act.wait_ge(d_free[job[0]], job[1] + 1)
                act.nop().then_inc(dp_ok, 2)

            def y_high(r, par):
                act.wait_ge(y_ok, r + 1)
                act.activation(yh[:, :, :], acc[:, par], ACT.Copy).then_inc(yh_ok, 1)

            def project(r):
                need(act, o_ok, CC * r)
                for c in range(CC):
                    for h in range(2):
                        job = BJ(r, 2 + 2 * c + h)
                        full(act, b_full, job)
                        act.activation(of[:, c, h * HALF:(h + 1) * HALF], pb[job[0]][:, 0:HALF], ACT.Identity,
                                       scale=1.0 / WS, bias=pbc[:, c:c + 1]).then_inc(b_free[job[0]], 1)
                        act.wait_ge(b_free[job[0]], job[1] + 1)
                    act.nop().then_inc(of_ok, 2)

            act.wait_ge(w_in, 64)
            act.activation(wh[:, :, :], wf[:, :, :], ACT.Copy, scale=WS).then_inc(w_hi, 1)
            act.wait_ge(pad_ok, 4)
            norm_root(0)
            norm(0, 0)
            norm_high(0, 0)

            def slot(s, par, half, kind):
                live, before = kind != "rest", kind != "first"
                if live:
                    values(s, par, before)
                elif before:
                    scale(s - 1)
                if live:
                    for j in range(NB):
                        v_pixels(s, j)
                    queries(s)
                    keys(s)
                    if kind in ("first", ""):
                        norm_root(s + 1)
                    queries_square(s)
                    keys_high(s)
                    queries_end(s)
                    depthwise(s, par, 0)
                if kind in ("first", ""):
                    norm(s + 1, 1 - par)
                    norm_high(s + 1, 1 - par)
                if before:
                    y_high(s - 1, 1 - par)
                if live:
                    product_high(s)
                    depthwise(s, par, 1)
                if before:
                    project(s - 1)
                if live:
                    attention(s)

            slots(act, slot)

        @block.vector
        def _(dve):
            chain = Tally(dv)

            def step(ins):
                chain.inc(ins)
                dve.wait_ge(dv, chain.value())

            def moments(s, par, half):
                dve.wait_ge(xb_in[par], 16 * (half + 1))
                for c in range(CC):
                    for h in range(2):
                        last = dve.bn_stats(bn[:, c, h], xb[:, par, c, h * HALF:(h + 1) * HALF])
                step(last)
                dve.nop().then_inc(bn_ok, 1)
                for c in range(CC):
                    last = dve.bn_aggr(mv[:, c], bn[:, c])
                step(last)
                step(dve.tensor_tensor(t1[:, :], mv[:, :, 0], mv[:, :, 0], ALU.mult))
                dve.tensor_tensor(mv[:, :, 1], mv[:, :, 1], t1[:, :], ALU.add).then_inc(rn_ok, 1)

            def statistics(s):
                for c in range(CC):
                    job = stat_job(s, c)
                    full(dve, b_full, job)
                    dve.tensor_copy(mt[:, c], pb[job[0]][:, 0:2]).then_inc(b_free[job[0]], 1)
                    dve.wait_ge(b_free[job[0]], job[1] + 1)
                step(dve.tensor_tensor(t2[:, :], mt[:, :, 0], mt[:, :, 0], ALU.mult))
                step(dve.tensor_tensor(sd[:, :], mt[:, :, 1], t2[:, :], ALU.subtract))
                dve.tensor_scalar(sd[:, :], sd[:, :], 0.0, None, ALU.max).then_inc(mv_ok, 1)

            def statistics_end(s):
                dve.wait_ge(sd_ok, s + 1)
                step(dve.reciprocal(r1[:, :], sd[:, :]))
                dve.scalar_tensor_tensor(n1[:, :], mt[:, :, 0], -1.0, r1[:, :], ALU.mult, ALU.mult).then_inc(mv_ok, 1)

            def pixels(s, j):
                job = A(s, KV + j)
                dve.wait_ge(vt_hi, NB * s + j + 1)
                dve.scalar_tensor_tensor(kf[:, j], pa[job[0]][0:NP, 0:C], 1.0 / WS, bkb[0:NP, 0:C], ALU.mult, ALU.add)
                dve.scalar_tensor_tensor(vtl[:, j, 0:C], pa[job[0]][0:NP, C:2 * C], 1.0 / WS, vth[:, j, 0:C],
                                         ALU.mult, ALU.subtract).then_inc(a_free[job[0]], 1)
                if j == NB - 1:
                    dve.wait_ge(a_free[job[0]], job[1] + 1)

            def keys(s):
                dve.tensor_scalar(kf[:, :, :], kf[:, :, :], 0.0, EPS, ALU.max, ALU.add).then_inc(kf_ok, 1)

            def keys_scale(s):
                dve.wait_ge(kn_ok, s + 1)
                step(dve.tensor_scalar(kr[:, :], kn[:, :], 1e-12, 1.0 / KS, ALU.max, ALU.mult))
                step(dve.reciprocal(kr[:, :], kr[:, :]))
                dve.tensor_tensor(kf[:, :, :], kf[:, :, :], kr[:, :].unsqueeze(2).to_broadcast([NP, NB, C]),
                                  ALU.mult).then_inc(kx_ok, 1)

            def keys_low(s):
                dve.wait_ge(kh_ok, s + 1)
                dve.tensor_tensor(kl[:, :, :], kf[:, :, :], kh[:, :, :], ALU.subtract).then_inc(kl_ok, 1)

            def product(s):
                for c in range(CC):
                    job = A(s, VK + c)
                    full(dve, a_full, job)
                    bank = pa[job[0]]
                    step(dve.tensor_copy(km[:, c:c + 1], bank[:, C:C + 1]))
                    dve.scalar_tensor_tensor(vk[:, c], bkb[:, C:2 * C], km[:, c:c + 1], bank[:, 0:C],
                                             ALU.mult, ALU.add).then_inc(vk_ok, 1)
                    dve.wait_ge(vk_ok, CC * s + c + 1)
                    dve.nop().then_inc(a_free[job[0]], 1)

            def product_low(s):
                for c in range(CC):
                    dve.wait_ge(vkh_ok, CC * s + c + 1)
                    dve.scalar_tensor_tensor(vkl[:, c], vk[:, c], 1.0 / (KS * N), vkh[:, c],
                                             ALU.mult, ALU.subtract).then_inc(vkl_ok, 1)

            def query_low(s):
                dve.wait_ge(th_ok, s + 1)
                dve.tensor_tensor(tl[:, :, :], tf[:, :, :], th[:, :, :], ALU.subtract).then_inc(tl_ok, 1)

            def taps(s, par, first, n):
                for t in range(first, min(first + n, VT)):
                    k, c = TAP_ORDER[t]
                    if k == KP:
                        dve.wait_ge(dp_ok, 4 * s + 2 * c + 2)
                    else:
                        dve.wait_ge(dv, chain.value() - (t - TAP_ORDER.index((k - 1, c)) - 1))
                    dy, dx = divmod(k, 5)
                    whole = acc[:, par, c].rearrange("p (a b) -> p a b", a=IMG)
                    chain.inc(dve.scalar_tensor_tensor(whole, vp[:, par, c, dy:dy + IMG, dx:dx + IMG], dw[:, c, k:k + 1],
                                                       whole, ALU.mult, ALU.add))

            def scaled(r, par):
                for h in range(2):
                    job = BJ(r, h)
                    full(dve, b_full, job)
                    for c in range(CC):
                        part = af[:, c, h * HALF:(h + 1) * HALF]
                        last = dve.scalar_tensor_tensor(part, part, col[:, 8 + c:9 + c], pb[job[0]][:, 0:HALF],
                                                        ALU.mult, ALU.mult)
                    last.then_inc(b_free[job[0]], 1)
                dve.wait_ge(b_free[1], BJ(r, 1)[1] + 1)
                dve.wait_ge(dv, chain.value())
                y = acc[:, par].rearrange("p c n -> p (c n)")
                dve.scalar_tensor_tensor(y, y, 1.0 / WS,
                                         af[:, :, :].rearrange("p c n -> p (c n)"), ALU.mult, ALU.add).then_inc(y_ok, 1)

            def y_low(r, par):
                dve.wait_ge(yh_ok, r + 1)
                dve.tensor_tensor(yl[:, :, :], acc[:, par], yh[:, :, :], ALU.subtract).then_inc(yl_ok, 1)

            def scale(s):
                full(dve, a_full, A(s, KZ))
                dve.wait_ge(a_free[SS % 4], A(s, SS)[1] + 1)
                step(dve.tensor_scalar(nn[:, :], nn[:, :], 1e-12, EPS, ALU.max, ALU.mult))
                dve.tensor_tensor(ww[:, :], nn[:, :], pa[KZ % 4][:, 0:Q], ALU.add).then_inc(a_free[KZ % 4], 1)
                dve.wait_ge(a_free[KZ % 4], A(s, KZ)[1] + 1)
                step(dve.scalar_tensor_tensor(nn[:, :], ww[:, :], EPS, ww[:, :], ALU.mult, ALU.mult))

            def scale_end(s):
                job = D(s, 4)
                full(dve, d_full, job)
                dve.tensor_tensor(ww[:, :], nn[:, :], pd[job[0]][:, 0:Q], ALU.add).then_inc(d_free[job[0]], 1)
                dve.wait_ge(d_free[job[0]], job[1] + 1)
                dve.nop().then_inc(ww_ok, 1)

            def scale_inverse(s):
                dve.wait_ge(fs_ok, s + 1)
                dve.reciprocal(sf[:, :], ww[:, :]).then_inc(sf_ok, 1)

            dve.memset(vp[:, :, :, :, :], 0.0).then_inc(pad_ok, 1)
            dve.memset(vh[:, :, :, :], 0.0)
            dve.memset(vl[:, :, :, :], 0.0).then_inc(pad_ok, 1)
            dve.memset(vth[:, :, C:C + 2], 1.0).then_inc(pad_ok, 1)
            dve.memset(vtl[:, :, C:C + 2], 0.0).then_inc(pad_ok, 1)
            dve.wait_ge(w_in, 64)
            step(dve.tensor_scalar(dw[:, :, :], dr[:, :, :], WS, None, ALU.mult))
            dve.wait_ge(w_hi, 1)
            dve.scalar_tensor_tensor(wl[:, :, :].rearrange("p c n -> p (c n)"), wf[:, :, :].rearrange("p c n -> p (c n)"), WS,
                                     wh[:, :, :].rearrange("p c n -> p (c n)"), ALU.mult, ALU.subtract).then_inc(w_ok, 1)
            for c in range(CC):
                for k in range(KP):
                    step(dve.tensor_scalar(dgf[:, :], idn, dw[:, c, k:k + 1], None, ALU.mult))
                    step(dve.tensor_copy(dgh[:, c, k], dgf[:, :]))
                    step(dve.tensor_tensor(dgl[:, c, k], dgf[:, :], dgh[:, c, k], ALU.subtract))
            dve.wait_ge(pb_ok, 1)
            for c in range(CC):
                dve.tensor_tensor(pbc[:, c:c + 1], pb[c][:, 0:1], col[:, 12 + c:13 + c], ALU.add).then_inc(dw_ok, 1)
            moments(0, 0, 0)
            statistics(0)
            statistics_end(0)

            def slot(s, par, half, kind):
                live, before = kind != "rest", kind != "first"
                r, rp = s - 1, 1 - par

                def rest(first, n):
                    if before:
                        taps(r, rp, first, n)

                if before:
                    scale_end(r)
                if kind in ("first", ""):
                    moments(s + 1, 1 - par, half + 1 if par else half)
                rest(EARLY, 3)
                if before and not live:
                    scale_inverse(r)
                if live:
                    for j in range(NB):
                        if before and j == 2:
                            scale_inverse(r)
                        pixels(s, j)
                        if j % 2:
                            rest(EARLY + 3 + j // 2, 1)
                    keys(s)
                    if kind in ("first", ""):
                        statistics(s + 1)
                    rest(EARLY + 6, 4)
                    keys_scale(s)
                    rest(EARLY + 10, 2)
                    keys_low(s)
                    rest(EARLY + 12, VT)
                    if kind in ("first", ""):
                        statistics_end(s + 1)
                else:
                    rest(EARLY + 3, VT)
                if before:
                    scaled(r, rp)
                if live:
                    query_low(s)
                if before:
                    y_low(r, rp)
                if live:
                    product(s)
                    product_low(s)
                if live:
                    taps(s, par, 0, 6)
                    scale(s)
                    taps(s, par, 6, EARLY - 6)

            slot(0, 0, 0, "first")
            slot(1, 1, 0, "")
            slot(2, 0, 1, "")
            with dve.Fori(1, B // 2 - 1) as t:
                chain.loop(t - 1, DV_LOOP)
                slot(2 * t + 1, 1, t, "")
                slot(2 * t + 2, 0, t + 1, "")
            chain.end(B // 2 - 2)
            slot(B - 1, 1, B // 2 - 1, "last")
            slot(B, 0, B // 2, "rest")

        @block.tensor
        def _(pe):
            def products(bank, terms, sync=None):
                for n, (w, m) in enumerate(terms):
                    last = pe.matmul(bank, w, m, start=(n == 0), stop=(n == len(terms) - 1))
                if sync is not None:
                    last.then_inc(sync, 1)

            def pairs(hi_w, lo_w, hi_m, lo_m):
                return ((hi_w, hi_m), (hi_w, lo_m), (lo_w, hi_m))

            def keys_values(s, par):
                for j in range(NB):
                    job = A(s, KV + j)
                    free(pe, a_free, job)
                    px = slice(NP * j, NP * j + NP)
                    products(pa[job[0]][0:NP, :], [t for c in range(CC) for t in pairs(
                        hh[:, par, c, px], hl[:, par, c, px], wh[:, c, C:3 * C], wl[:, c, C:3 * C])], a_full[job[0]])

            def channels(s, par, first, w0, blocks=(0, 1, 2, 3)):
                for m in range(CC):
                    for h in range(2):
                        if 2 * m + h not in blocks:
                            continue
                        job = A(s, first + 2 * m + h)
                        free(pe, a_free, job)
                        px, wc = slice(HALF * h, HALF * h + HALF), slice(w0 + P * m, w0 + P * m + P)
                        products(pa[job[0]][:, 0:HALF], [t for c in range(CC) for t in pairs(
                            wh[:, c, wc], wl[:, c, wc], hh[:, par, c, px], hl[:, par, c, px])], a_full[job[0]])

            def product(s):
                pe.wait_ge(kl_ok, s + 1)
                for c in range(CC):
                    job = A(s, VK + c)
                    free(pe, a_free, job)
                    ch = slice(P * c, P * c + P)
                    products(pa[job[0]][:, 0:C + 1], [t for j in range(NB) for t in pairs(
                        kh[:, j, ch], kl[:, j, ch], vth[:, j, 0:C + 1], vtl[:, j, 0:C + 1])], a_full[job[0]])

            def quarters(banks, sem_full, sem_free, job, weight, moving):
                free(pe, sem_free, job)
                for q in range(4):
                    for c in range(CC):
                        last = pe.matmul(banks[job[0]][32 * q:32 * q + 32, 0:Q], weight(c), moving[:, c, Q * q:Q * q + Q],
                                         start=(c == 0), stop=(c == CC - 1))
                last.then_inc(sem_full[job[0]], 1)

            def attention(s):
                for m in range(CC):
                    for h in range(2):
                        job = A(s, AT + 2 * m + h)
                        free(pe, a_free, job)
                        px, ch = slice(HALF * h, HALF * h + HALF), slice(P * m, P * m + P)
                        products(pa[job[0]][:, 0:HALF], [t for c in range(CC) for t in pairs(
                            vkh[:, c, ch], vkl[:, c, ch], th[:, c, px], tl[:, c, px])], a_full[job[0]])

            def depthwise(s, c, h):
                job = D(s, 2 * c + h)
                free(pe, d_free, job)
                win = lambda v, k: v[:, c, h * HR + k // 5:h * HR + k // 5 + HR, k % 5:k % 5 + IMG]
                products(pd[job[0]][:, 0:HALF], [t for k in range(KP) for t in pairs(
                    dgh[:, c, k], dgl[:, c, k], win(vh, k), win(vl, k))], d_full[job[0]])

            def statistics(s):
                pe.wait_ge(rn_ok, s + 1)
                for c in range(CC):
                    job = stat_job(s, c)
                    free(pe, b_free, job)
                    products(pb[job[0]][:, 0:2], [(gavg, mv[:, c])], b_full[job[0]])

            def spread(r):
                pe.wait_ge(sf_ok, r + 1)
                for h in range(2):
                    job = BJ(r, h)
                    free(pe, b_free, job)
                    for k in range(2):
                        last = pe.matmul(pb[job[0]][:, Q * k:Q * k + Q], sl[:, 2 * h + k], sf[:, :],
                                         start=(k == 0), stop=True, skip_group_check=True)
                    last.then_inc(b_full[job[0]], 1)

            def project(r):
                pe.wait_ge(yl_ok, r + 1)
                for m in range(CC):
                    for h in range(2):
                        job = BJ(r, 2 + 2 * m + h)
                        free(pe, b_free, job)
                        px, wc = slice(HALF * h, HALF * h + HALF), slice(3 * C + P * m, 3 * C + P * m + P)
                        products(pb[job[0]][:, 0:HALF], [t for c in range(CC) for t in pairs(
                            wh[:, c, wc], wl[:, c, wc], yh[:, c, px], yl[:, c, px])], b_full[job[0]])

            pe.wait_ge(w_in, 64)
            for m in range(CC):
                products(pb[m][:, 0:1], [(wf[:, c, 3 * C + P * m:3 * C + P * m + P], col[:, 10 + c:11 + c])
                                         for c in range(CC)], pb_ok if m else None)
            pe.wait_ge(dw_ok, 2)
            statistics(0)
            pe.wait_ge(w_ok, 1)

            def slot(s, par, half, kind):
                live, before = kind != "rest", kind != "first"
                if live:
                    pe.wait_ge(hl_ok, s + 1)
                    channels(s, par, V, 2 * C, (0, 1))
                if before:
                    pe.wait_ge(asq_ok, s)
                    quarters(pd, d_full, d_free, D(s - 1, 4), lambda c: mean_ch, sq)
                if live:
                    channels(s, par, V, 2 * C, (2, 3))
                    keys_values(s, par)
                if kind in ("first", ""):
                    statistics(s + 1)
                if live:
                    channels(s, par, QJ, 0)
                if before:
                    spread(s - 1)
                if live:
                    pe.wait_ge(vl_ok, CC * s + CC)
                    depthwise(s, 0, 0)
                    depthwise(s, 0, 1)
                    product(s)
                    depthwise(s, 1, 0)
                    depthwise(s, 1, 1)
                if before:
                    project(s - 1)
                if live:
                    pe.wait_ge(tsq_ok, s + 1)
                    quarters(pa, a_full, a_free, A(s, SS), lambda c: ones, sq)
                    pe.wait_ge(kmb_ok, CC * s + CC)
                    quarters(pa, a_full, a_free, A(s, KZ), lambda c: kmb[:, c], tf)
                    pe.wait_ge(tl_ok, s + 1)
                    pe.wait_ge(vkl_ok, CC * s + CC)
                    attention(s)

            slots(pe, slot)


_VECTORS = ["L0_conv_bias", "L1_conv_qkv_b", "L1_conv_qkv_b", "L1_conv_norm_w", "L1_conv_dwc_b", "L1_conv_proj_b"]
_FIRST = [0, 0, 2 * C, 0, 0, 0]


def _constants(np):
    group = np.kron(np.eye(P // GN), np.full((GN, GN), 1.0 / GN)).astype(np.float32)
    mask = np.tile(np.eye(JB) * GSC, (NE, 1)).astype(np.float32)
    l1c = np.zeros((P, 6 * P), np.float32)
    for q in range(4):
        l1c[32 * q, q * P:(q + 1) * P] = 1.0
    l1c[:, 4 * P:5 * P] = np.eye(P)
    for k, v in enumerate((1.0, 1.0 / C, 1.0 / (KS * N))):
        l1c[:, 5 * P + 32 * k:5 * P + 32 * k + 32] = v
    return group, mask, l1c


def kernel(**inputs):
    import numpy as np
    import concourse.bacc as bacc
    from concourse.bass_utils import run_bass_kernel_spmd

    a = {k: np.asarray(v) for k, v in inputs.items()}
    group, mask, l1c = _constants(np)
    rw = a["L0_conv_route_w"].reshape(NE, CC, P).transpose(2, 1, 0)
    route = np.concatenate([np.repeat(rw, JB, axis=2).reshape(P, CC * P), mask], axis=1)
    wmix = a["L0_conv_weight"].reshape(2, P // JB, JB, CC, P, 9, NE).transpose(0, 3, 5, 6, 2, 1, 4).reshape(2 * U, P, P * P // JB)
    cols = [np.full((P, 1), EPS, np.float32), np.repeat(a["L0_conv_route_b"], JB).reshape(P, 1)]
    for name, first in zip(_VECTORS, _FIRST):
        cols.append(a[name][first:first + C].reshape(CC, P).T)
    lw = np.concatenate([a["L1_conv_qkv_w"], a["L1_conv_proj_w"]], axis=0).T.reshape(CC, P, 4 * C).transpose(1, 0, 2)
    data = {
        "x": a["x"], "route": route, "wmix": wmix, "consts": group, "cols": np.concatenate(cols, axis=1), "lw": lw,
        "rows": np.broadcast_to(a["L1_conv_qkv_b"][C:3 * C], (P, 2 * C)), "l1c": l1c,
        "dwc": a["L1_conv_dwc_w"].reshape(CC, P, TAPS).transpose(1, 0, 2),
    }
    nc = bacc.Bacc("TRN2", target_bir_lowering=False, num_devices=1)
    data = {k: np.ascontiguousarray(v) for k, v in data.items()}
    args = {k: nc.dram_tensor(f"in_{k}", v.shape, F32, kind="ExternalInput").ap() for k, v in data.items()}
    wpair = nc.dram_tensor("wpair", (2 * U, P, 2 * P * P // JB), F16).ap()
    x1s = nc.dram_tensor("x1s", (B, CC, P, N), F32).ap()
    out = nc.dram_tensor("out", (B, C, IMG, IMG), F32, kind="ExternalOutput").ap()
    mk_conv_preact(nc, wpair=wpair, x1s=x1s, out=out, **args)
    r = run_bass_kernel_spmd(nc, [{f"in_{k}": v for k, v in data.items()}], core_ids=[0])
    return r.results[0]["out"]
```

```python
import concourse.bass as bass
from concourse import mybir
from contextlib import ExitStack

F32 = mybir.dt.float32
F32R = mybir.dt.float32r
F16 = mybir.dt.float16
ALU = mybir.AluOpType
ACT = mybir.ActivationFunctionType
AX = mybir.AxisListType

P = 128
B, C, IMG = 32, 256, 28
CC = C // P
N = IMG * IMG
HALF = N // 2
HR = IMG // 2
NE = 8
JB = P // NE
GS = 4
NG = B // GS
PH = 4
U = PH * CC * 3
TR = 2 * CC * 3
TW = IMG // 2
NT = IMG * TW
GN = 8
EPS = 1e-5
WS = 1024.0
GSC = 16.0
PAD1 = IMG + 2
KCH = U // GS
BANKS = PH
WR = 3
WB = 3
XR = 8
TAPS = 25
KW = 5
PX = (0, 1, 2)
VX = (3, 4)
FC = 32
FP = P // FC
FJ = (IMG + KW - 1) // FP
FO = IMG // FP
FB = 2
NB = 7
NP = N // NB
Q = N // 4
KS = 64.0
PAD2 = IMG + 4
LEAD = 4
V_TAPS = [KW * dy + dx for dx in VX for dy in range(KW)]
TAP_ORDER = [(k, 0) for k in V_TAPS[:LEAD]] + [
    (V_TAPS[n], c) for m in range(len(V_TAPS)) for c, n in ((1, m), (0, m + LEAD)) if n < len(V_TAPS)]
VT = len(TAP_ORDER)
FIRST = 3
EARLY = 9
DV_LOOP = 2 * (VT + 12)


class Tally:

    def __init__(self, sem):
        self.sem, self.total, self.local, self.i, self.per = sem, 0, 0, None, 0

    def loop(self, i, per):
        self.i, self.per, self.local = i, per, 0

    def end(self, turns):
        assert self.local == self.per, (self.local, self.per)
        self.total += self.per * turns
        self.i = None

    def inc(self, ins, n=1):
        ins.then_inc(self.sem, n)
        if self.i is None:
            self.total += n
        else:
            self.local += n

    def value(self):
        return self.total if self.i is None else self.i * self.per + (self.total + self.local)


def need(eng, sem, value):
    if isinstance(value, int) and value <= 0:
        return
    eng.wait_ge(sem, value)


def mk_conv_preact(nc, x, route, wmix, consts, cols, lw, rows, l1c, dwc, dwb, wpair, x1s, vdram, adram, out):
    xv = x.rearrange("b (c p) h w -> b p c (h w)", c=CC)
    with ExitStack() as outer:
        def keep(kind, name, shape, dt=None):
            if kind == "sem":
                return outer.enter_context(nc.semaphore(name))
            return outer.enter_context(nc.sbuf_tensor(name, shape, dt))

        cst = keep("sb", "cst", [P, P], F32)
        col = keep("sb", "col", [P, cols.shape[1]], F32)
        rs = keep("sb", "rs", [P, B * CC], F32)
        nb = keep("sb", "nb", [P, B * CC], F32)
        bdh = keep("sb", "bdh", [P, B * JB], F16)
        bdl = keep("sb", "bdl", [P, B * JB], F16)
        gavg = cst[:, 0:P]
        eps = col[:, 0:1]

        prologue(nc, xv, route, wmix, consts, cols, wpair, cst, col, gavg, eps, rs, nb, bdh, bdl)
        routed_conv(nc, xv, wpair, x1s, col, rs, nb, bdh, bdl)
        if out is not None:
            linear_attention(nc, x1s, out, lw, rows, l1c, cst, col, dwc, dwb, vdram, adram)


def prologue(nc, xv, route, wmix, consts, cols, wpair, cst, col, gavg, eps, rs, nb, bdh, bdl):
    with ExitStack() as ctx:
        sb = lambda n, s, d: ctx.enter_context(nc.sbuf_tensor(n, s, d))
        sem = lambda n: ctx.enter_context(nc.semaphore(n))
        M = P * P // JB
        wf = sb("wf", [P, WB, 3, M], F32)
        ws = sb("ws", [P, WB, 2, M], F32)
        wp = sb("wp", [P, WB, PH, 2, M], F16)
        xs = sb("xs", [P, XR, CC, N], F32)
        bn = sb("bn", [P, B, CC, 2, 6], F32)
        mv = sb("mv", [P, B * CC, 2], F32)
        mt = sb("mt", [P, B * CC, 2], F32)
        tmp = sb("tmp", [P, B * CC], F32)
        tm2 = sb("tm2", [P, B * CC], F32)
        std = sb("std", [P, B * CC], F32)
        se = sb("se", [P, B, CC], F32)
        rw = sb("rw", [P, CC, P], F32)
        gate = sb("gate", [P, B], F32)
        hb = sb("hb", [P, 1], F32)
        mask = sb("mask", [P, JB], F32)
        bdf = sb("bdf", [P, B, JB], F32)
        pstat = ctx.enter_context(nc.psum_tensor("pstat", [P, 512], F32))
        pgate = ctx.enter_context(nc.psum_tensor("pgate", [P, 512], F32))
        small_in = sem("small_in")
        w_in = [sem(f"w_in{i}") for i in range(WB)]
        w_out = [sem(f"w_out{i}") for i in range(WB)]
        outer_sum, w_sum = sem("outer_sum"), sem("w_sum")
        x_in = [sem(f"x_in{i}") for i in range(XR)]
        w_hi, w_lo = sem("w_hi"), sem("w_lo")
        stats = sem("stats")
        stat_pe, gate_pe, std_ok, gate_ok, v_step = sem("stat_pe"), sem("gate_pe"), sem("std_ok"), sem("gate_ok"), sem("v_step")
        block = ctx.enter_context(nc.Block())

        def images(n):
            return range(B * n // TR, B * (n + 1) // TR)

        def parts(n):
            return ((0, wf[:, n % WB, 0], WS), (3, wf[:, n % WB, 2], WS), (1, ws[:, n % WB, 0], WS / 2), (2, ws[:, n % WB, 1], WS / 2))

        @block.sync
        def _(sp):
            sp.dma_start(cst[:, :], consts).then_inc(small_in, 16)
            sp.dma_start(col[:, :], cols).then_inc(small_in, 16)
            sp.dma_start(rw[:, :, :], route[:, 0:CC * P].rearrange("p (c m) -> p c m", c=CC)).then_inc(small_in, 16)
            sp.dma_start(mask[:, :], route[:, CC * P:CC * P + JB]).then_inc(small_in, 16)
            for n in range(TR):
                need(sp, w_lo, PH * (n - WB + 1))
                sp.dma_start(wf[:, n % WB], wmix[3 * n:3 * n + 3].rearrange("t p m -> p t m")).then_inc(w_in[n % WB], 16)
                for i in images(n):
                    need(sp, stats, i - XR + 1)
                    sp.dma_start(xs[:, i % XR], xv[i]).then_inc(x_in[i % XR], 16)

        @block.gpsimd
        def _(pool):
            def store(n):
                pool.wait_ge(w_lo, PH * n + PH)
                H, cy = divmod(n, CC * 3)
                pool.dma_start(wpair[H, :, cy].rearrange("k p m -> p k m"),
                               wp[:, n % WB].rearrange("p k a m -> p k (a m)")).then_inc(w_out[n % WB], 16)

            for n in range(TR):
                pool.wait_ge(w_in[n % WB], 16 * (n // WB + 1))
                need(pool, w_lo, PH * (n - WB + 1))
                pool.tensor_tensor(ws[:, n % WB, 1], wf[:, n % WB, 0], wf[:, n % WB, 2], ALU.add).then_inc(outer_sum, 1)
                if n:
                    store(n - 1)
            store(TR - 1)
            for k in range(WB):
                pool.wait_ge(w_out[k], 16 * (TR // WB))

        @block.scalar
        def _(act):
            for n in range(TR):
                act.wait_ge(w_in[n % WB], 16 * (n // WB + 1))
                if n >= WB:
                    act.wait_ge(w_out[n % WB], 16 * (n // WB))
                for k, src, scale in parts(n):
                    if k == 1:
                        act.wait_ge(w_sum, 2 * n + 2)
                    act.activation(wp[:, n % WB, k, 0], src, ACT.Copy, scale=scale).then_inc(w_hi, 1)
            act.wait_ge(small_in, 64)
            act.wait_ge(v_step, 5)
            act.activation(std[:, :], tmp[:, :], ACT.Sqrt).then_inc(std_ok, 1)
            act.wait_ge(gate_pe, 1)
            act.wait_ge(v_step, 13)
            act.activation(gate[:, :], pgate[:, 0:B], ACT.Tanh, scale=0.5, bias=hb[:, :]).then_inc(gate_ok, 1)

        @block.vector
        def _(dve):
            steps = Tally(v_step)

            def step(ins):
                steps.inc(ins)
                dve.wait_ge(v_step, steps.value())

            for n in range(TR):
                dve.wait_ge(outer_sum, n + 1)
                dve.tensor_tensor(ws[:, n % WB, 0], ws[:, n % WB, 1], wf[:, n % WB, 1], ALU.add).then_inc(w_sum, 1)
                dve.tensor_tensor(ws[:, n % WB, 1], ws[:, n % WB, 1], wf[:, n % WB, 1], ALU.subtract).then_inc(w_sum, 1)
                for i in images(n):
                    k = i % XR
                    dve.wait_ge(x_in[k], 16 * (i // XR + 1))
                    for c in range(CC):
                        for h in range(2):
                            last = dve.bn_stats(bn[:, i, c, h], xs[:, k, c, h * HALF:(h + 1) * HALF])
                    last.then_inc(stats, 1)
                for j, (k, src, scale) in enumerate(parts(n)):
                    dve.wait_ge(w_hi, PH * n + j + 1)
                    dve.scalar_tensor_tensor(wp[:, n % WB, k, 1], src, scale, wp[:, n % WB, k, 0],
                                             ALU.mult, ALU.subtract).then_inc(w_lo, 1)
                dve.wait_ge(stats, images(n)[-1] + 1)
                for i in images(n):
                    for c in range(CC):
                        last = dve.bn_aggr(mv[:, i * CC + c], bn[:, i, c])
            mean, sq = mv[:, :, 0], mv[:, :, 1]
            step(last)
            step(dve.tensor_tensor(tmp[:, :], mean, mean, ALU.mult))
            step(dve.tensor_tensor(sq, sq, tmp[:, :], ALU.add))
            dve.wait_ge(stat_pe, 1)
            step(dve.tensor_copy(mt[:, :, :], pstat[:, 0:2 * B * CC].rearrange("p (a b) -> p a b", b=2)))
            dve.tensor_tensor(tm2[:, :], mt[:, :, 0], mt[:, :, 0], ALU.mult).then_inc(stats, 1)
            dve.wait_ge(stats, B + 1)
            dve.tensor_tensor(tmp[:, :], mt[:, :, 1], tm2[:, :], ALU.subtract).then_inc(stats, 1)
            dve.wait_ge(stats, B + 2)
            step(dve.tensor_scalar(tmp[:, :], tmp[:, :], 0.0, EPS, ALU.max, ALU.add))
            dve.wait_ge(std_ok, 1)
            step(dve.reciprocal(rs[:, :], std[:, :]))
            step(dve.tensor_tensor(tm2[:, :], rs[:, :], rs[:, :], ALU.mult))
            step(dve.scalar_tensor_tensor(tm2[:, :], tmp[:, :], -0.5, tm2[:, :], ALU.mult, ALU.mult))
            step(dve.scalar_tensor_tensor(rs[:, :], tm2[:, :], 1.5, rs[:, :], ALU.add, ALU.mult))
            step(dve.scalar_tensor_tensor(nb[:, :], mt[:, :, 0], -1.0, rs[:, :], ALU.mult, ALU.mult))
            step(dve.tensor_tensor(tm2[:, :], mean, rs[:, :], ALU.mult))
            step(dve.tensor_tensor(se[:, :, :].rearrange("p b c -> p (b c)"), tm2[:, :], nb[:, :], ALU.add))
            step(dve.tensor_scalar(hb[:, :], col[:, 1:2], 0.5, None, ALU.mult))
            dve.wait_ge(gate_ok, 1)
            step(dve.tensor_scalar(gate[:, :], gate[:, :], 0.5, 0.5, ALU.mult, ALU.add))
            step(dve.tensor_tensor(bdf[:, :, :], gate[:, :].unsqueeze(2).to_broadcast([P, B, JB]),
                                   mask[:, :].unsqueeze(1).to_broadcast([P, B, JB]), ALU.mult))
            bd = bdf[:, :, :].rearrange("p b j -> p (b j)")
            step(dve.tensor_copy(bdh[:, :], bd))
            step(dve.tensor_tensor(bdl[:, :], bd, bdh[:, :], ALU.subtract))

        @block.tensor
        def _(pe):
            pe.wait_ge(small_in, 64)
            pe.wait_ge(v_step, 3)
            pe.matmul(pstat[:, 0:2 * B * CC], gavg, mv[:, :, :].rearrange("p a b -> p (a b)"),
                      start=True, stop=True).then_inc(stat_pe, 1)
            pe.wait_ge(v_step, 12)
            for c in range(CC):
                last = pe.matmul(pgate[:, 0:B], rw[:, c], se[:, :, c], start=(c == 0), stop=(c == CC - 1))
            last.then_inc(gate_pe, 1)


def routed_conv(nc, xv, wpair, x1s, col, rs, nb, bdh, bdl):
    with ExitStack() as ctx:
        sb = lambda n, s, d: ctx.enter_context(nc.sbuf_tensor(n, s, d))
        sem = lambda n: ctx.enter_context(nc.semaphore(n))
        wdh = sb("wdh", [P, 2, GS, U, P], F16)
        wdl = sb("wdl", [P, 2, GS, U, P], F16)
        wr = sb("wr", [P, WR, 2, 1024], F16)
        xg = sb("xg", [P, GS, CC, N], F32)
        xh = sb("xh", [P, GS, CC, PH, PAD1, TW], F16)
        xl = sb("xl", [P, GS, CC, PH, PAD1, TW], F16)
        xf = sb("xf", [P, CC, IMG, PAD1], F32)
        xw = sb("xw", [P, PH, IMG, TW], F32)
        bg = sb("bg", [P, 2, GS * JB], F16)
        pm = [ctx.enter_context(nc.psum_tensor(f"pm{k}", [P, 512], F32)) for k in range(4)]
        pc = [ctx.enter_context(nc.psum_tensor(f"pc{k}", [P, 512], F32)) for k in range(4)]
        w_in = [sem(f"wr_in{k}") for k in range(WR)]
        x_in = [sem(f"xg_in{k}") for k in range(GS)]
        x1_out = [sem(f"x1_out{k}") for k in range(GS)]
        mixed, mix_hi, mix_lo = sem("mixed"), sem("mix_hi"), sem("mix_lo")
        conv_done, conv_out = sem("conv_done"), sem("conv_out")
        bg_ok, xf_ok, xw_ok, xh_ok, xl_ok, xb_ok = sem("bg_ok"), sem("xf_ok"), sem("xw_ok"), sem("xh_ok"), sem("xl_ok"), sem("xb_ok")
        block = ctx.enter_context(nc.Block())

        def over_groups(eng, body):
            with eng.Fori(0, NG - 1) as g:
                body(g, False)
            body(NG - 1, True)

        def chunk(g, H, u):
            return 2 * U * g + U * H + u

        def job(g, H, i):
            return PH * (2 * GS * g + GS * H + i)

        def chunks(i):
            return range(KCH * i, KCH * i + KCH)

        def slots(eng, slot):
            def body(g, last):
                for H in range(2):
                    for i in range(GS):
                        ready = None
                        if not H and i < 2:
                            ready = (g, i + 2)
                        elif H and i >= 2 and not last:
                            ready = (g + 1, i - 2)
                        mixes = [(g + H, 1 - H, u) for u in chunks(i)] if not (last and H) else [None] * KCH
                        slot(g, H, i, last, mixes, ready)

            over_groups(eng, body)

        @block.sync
        def _(sp):
            def load_w(g, H, u):
                n = chunk(g, H, u)
                need(sp, mixed, n - WR + 1)
                sp.dma_start(wr[:, u % WR].rearrange("p k f -> p (k f)"), wpair[H, u // (CC * 3), u % (CC * 3)]).then_inc(w_in[u % WR], 16)

            def load_x(g, i):
                if not isinstance(g, int) or g:
                    sp.wait_ge(x1_out[i], 32 * g)
                s = GS * g + i
                src = xv[s] if isinstance(s, int) else xv[bass.ds(s, 1)].rearrange("a p c n -> (a p) c n")
                sp.dma_start(xg[:, i], src).then_inc(x_in[i], 16)

            def store(g, H, i):
                sp.wait_ge(conv_out, BANKS + job(g, H, i) + PH)
                s = GS * g + i
                dst = x1s[s, H] if isinstance(s, int) else x1s[bass.ds(s, 1), H].rearrange("a p n -> (a p) n")
                sp.dma_start(dst, xg[:, i, H]).then_inc(x1_out[i], 16)

            for u in range(U):
                load_w(0, 0, u)
                if u % 4 == 3 and u // 4 < GS:
                    load_x(0, u // 4)

            def load_first(g):
                for u in range(2):
                    load_w(g, 1, u)

            load_first(0)

            def slot(g, H, i, last, mixes, ready):
                for n, m in enumerate(mixes):
                    if m and (H or i or n > 1):
                        load_w(*m)
                    if n == 1:
                        if i:
                            store(g, H, i - 1)
                        elif H:
                            store(g, 0, GS - 1)
                        if H and i and not last:
                            load_x(g + 1, i - 1)
                if H and i == GS - 1:
                    if not last:
                        load_first(g + 1)
                    store(g, 1, GS - 1)
                    if not last:
                        load_x(g + 1, GS - 1)

            slots(sp, slot)
            for i in range(GS):
                sp.wait_ge(x1_out[i], 32 * NG)

        @block.gpsimd
        def _(pool):
            def low(g, i):
                s = GS * g + i
                for c in range(CC):
                    pool.wait_ge(xh_ok, 2 * s + c + 1)
                    pool.tensor_tensor(xl[:, i, c, :, 1:1 + IMG, :], xw[:, :, :, :],
                                       xh[:, i, c, :, 1:1 + IMG, :], ALU.subtract).then_inc(xl_ok, 1)

            def slot(g, H, i, last, mixes, ready):
                if ready:
                    low(*ready)

            for i in range(2):
                low(0, i)
            slots(pool, slot)

        @block.scalar
        def _(act):
            def normal(g, i):
                s = GS * g + i
                act.wait_ge(x_in[i], 16 * g + 16)
                if isinstance(g, int) and g == 0:
                    act.wait_ge(conv_out, BANKS)
                for c in range(CC):
                    need(act, xw_ok, 2 * s + c - 1)
                    k = CC * s + c
                    sc = rs[:, k:k + 1] if isinstance(k, int) else rs[:, bass.ds(k, 1)]
                    bi = nb[:, k:k + 1] if isinstance(k, int) else nb[:, bass.ds(k, 1)]
                    act.activation(xf[:, c, :, 1:1 + IMG], xg[:, i, c].rearrange("p (a b) -> p a b", a=IMG), ACT.Identity,
                                   scale=sc, bias=bi).then_inc(xf_ok, 1)

            def high(g, i, c):
                act.wait_ge(xw_ok, 2 * (GS * g + i) + c + 1)
                act.activation(xh[:, i, c, :, 1:1 + IMG, :], xw[:, :, :, :], ACT.Copy).then_inc(xh_ok, 1)

            def biased(g, i):
                act.wait_ge(xf_ok, 2 * (GS * g + i) + 2)
                for c in range(CC):
                    act.activation(xg[:, i, c], xg[:, i, c], ACT.Identity, bias=col[:, 2 + c:3 + c]).then_inc(xb_ok, 1)

            def mix(g, H, u):
                n = chunk(g, H, u)
                act.wait_ge(mixed, n + 1)
                act.activation(wdh[:, H, :, u, :], pm[u % 4][:, :].rearrange("p (b m) -> p b m", b=GS),
                               ACT.Copy, scale=1.0 / GSC).then_inc(mix_hi, 1)

            def gates(g):
                if not (isinstance(g, int) and g == 0):
                    act.wait_ge(mixed, 2 * U * g)
                for k, src in enumerate((bdh, bdl)):
                    part = src[:, 0:GS * JB] if isinstance(g, int) and g == 0 else src[:, bass.ds(GS * JB * g, GS * JB)]
                    act.activation(bg[:, k], part, ACT.Copy).then_inc(bg_ok, 1)

            def slot(g, H, i, last, mixes, ready):
                if H and i == 0 and not last:
                    gates(g + 1)
                for n, m in enumerate(mixes):
                    if m:
                        mix(*m)
                    if ready and n == 0:
                        normal(*ready)
                    if ready and n == 1:
                        high(*ready, 0)
                    if ready and n == 2:
                        biased(*ready)
                    if ready and n == 5:
                        high(*ready, 1)

            gates(0)
            for u in range(U):
                mix(0, 0, u)
                if u == 10:
                    normal(0, 0)
                if u == 12:
                    high(0, 0, 0)
                if u == 16:
                    high(0, 0, 1)
                    biased(0, 0)
            for i in range(1, 2):
                normal(0, i)
                high(0, i, 0)
                high(0, i, 1)
                biased(0, i)
            slots(act, slot)

        @block.vector
        def _(dve):
            dve.memset(xf[:, :, :, 0:PAD1:PAD1 - 1], 0.0)
            for tile in (xh, xl):
                for i in range(0, GS, 2):
                    edge = tile[:, i:i + 2].rearrange("p i c k a b -> p (i c k) a b")[:, :, 0:PAD1:PAD1 - 1, :]
                    dve.memset(edge, 0.0).then_inc(conv_out, 1)

            def mix(g, H, u):
                n = chunk(g, H, u)
                dve.wait_ge(mix_hi, n + 1)
                dve.scalar_tensor_tensor(wdl[:, H, :, u, :], pm[u % 4][:, :].rearrange("p (b m) -> p b m", b=GS),
                                         1.0 / GSC, wdh[:, H, :, u, :], ALU.mult, ALU.subtract).then_inc(mix_lo, 1)

            def add(g, H, i, k):
                if H == 0 and k == 0:
                    dve.wait_ge(xb_ok, 2 * (GS * g + i) + 2)
                pixels = xg[:, i, H].rearrange("p (n two) -> p n two", two=2)
                dve.wait_ge(conv_done, job(g, H, i) + k + 1)
                dve.wait_ge(conv_out, BANKS + job(g, H, i) + k)
                signs = ((1, 0), (1, 1), (1, -1), (0, -1))[k]
                for odd in range(2):
                    if signs[odd]:
                        last = dve.scalar_tensor_tensor(pixels[:, :, odd], pc[k][:, 0:NT], signs[odd] / WS,
                                                        pixels[:, :, odd], ALU.mult, ALU.add)
                last.then_inc(conv_out, 1)

            def transform(g, i, c):
                n = 2 * (GS * g + i) + c
                dve.wait_ge(xf_ok, n + 1)
                need(dve, xh_ok, n)
                need(dve, xl_ok, n)
                d = [xf[:, c, :, k:k + 2 * TW - 1:2] for k in range(PH)]
                for k, (a, b, op) in enumerate(((d[0], d[2], ALU.subtract), (d[1], d[2], ALU.add),
                                                (d[2], d[1], ALU.subtract), (d[1], d[3], ALU.subtract))):
                    last = dve.tensor_tensor(xw[:, k], a, b, op)
                last.then_inc(xw_ok, 1)

            def slot(g, H, i, last, mixes, ready):
                for n, m in enumerate(mixes):
                    if n == 2:
                        add(g, H, i, 1)
                    if n == 5:
                        add(g, H, i, 3)
                    if m:
                        mix(*m)
                    if n == 0:
                        add(g, H, i, 0)
                    if n == 3:
                        add(g, H, i, 2)
                    if ready and n in (1, 4):
                        transform(*ready, n // 3)

            for u in range(U):
                mix(0, 0, u)
                if u in (11, 15):
                    transform(0, 0, (u - 11) // 4)
            for i in range(1, 2):
                transform(0, i, 0)
                transform(0, i, 1)
            slots(dve, slot)

        @block.tensor
        def _(pe):
            def mix(g, H, u):
                n = chunk(g, H, u)
                if u == 0 and H == 0:
                    pe.wait_ge(bg_ok, 2 * g + 2)
                pe.wait_ge(w_in[u % WR], 16 * (2 * U // WR * g + U // WR * H + u // WR + 1))
                need(pe, mix_lo, n - 3)
                bank = pm[u % 4][:, :].rearrange("p (b m) -> p b m", b=GS)
                for jb in range(8):
                    dst = bank[:, :, jb * JB:(jb + 1) * JB]
                    for k, (wk, gk) in enumerate(((0, 0), (0, 1), (1, 0))):
                        last = pe.matmul(dst, wr[:, u % WR, wk, jb * P:(jb + 1) * P],
                                         bg[:, gk].rearrange("p (b j) -> p b j", b=GS),
                                         start=(k == 0 and jb == 0), stop=(k == 2), skip_group_check=True)
                last.then_inc(mixed, 1)

            def conv(g, H, i, after):
                pe.wait_ge(mix_lo, chunk(g, H, U))
                pe.wait_ge(xl_ok, 2 * (GS * g + i) + 2)
                for u in range(U):
                    k, (c, dy) = u // (CC * 3), divmod(u % (CC * 3), 3)
                    if c == dy == 0:
                        pe.wait_ge(conv_out, job(g, H, i) + k + 1)
                    for wk, xk in ((wdh, xh), (wdh, xl), (wdl, xh)):
                        last = pe.matmul(pc[k][:, 0:NT], wk[:, H, i, u, :], xk[:, i, c, k, dy:dy + IMG, :],
                                         start=(c == dy == 0 and wk is wdh and xk is xh),
                                         stop=(c == CC - 1 and dy == 2 and wk is wdl))
                    if c == CC - 1 and dy == 2:
                        last.then_inc(conv_done, 1)
                    if u in after:
                        mix(*after[u])

            for u in range(U):
                mix(0, 0, u)

            def slot(g, H, i, last, mixes, ready):
                conv(g, H, i, {GS * n + GS - 1: m for n, m in enumerate(mixes) if m})

            slots(pe, slot)


def linear_attention(nc, x1s, out, lw, rows, l1c, cst, col, dwc, dwb, vdram, adram):
    ov = out.rearrange("b (c p) h w -> b p c (h w)", c=CC)
    eps, gavg = col[:, 0:1], cst[:, 0:P]
    with ExitStack() as ctx:
        sb = lambda n, s, d=F32: ctx.enter_context(nc.sbuf_tensor(n, s, d))
        sem = lambda n: ctx.enter_context(nc.semaphore(n))
        wf = sb("wf1", [P, CC, 4 * C])
        wh = sb("wh", [P, CC, 4 * C], F16)
        wl = sb("wl", [P, CC, 4 * C], F16)
        bkb = sb("bkb", [P, 2 * C])
        kc = sb("kc", [P, 6 * P])
        dr = sb("dr", [P, CC, TAPS])
        dw = sb("dw", [P, CC, TAPS])
        NM = len(PX) * FB
        bw = sb("bw", [P, CC * FP, NM * FP])
        bdm = wf[:, 0, 0:NM * P]
        bmh = sb("bmh", [P, CC * FP, NM, P], F16)
        bml = sb("bml", [P, CC * FP, NM, P], F16)
        pbc = sb("pbc", [P, CC])
        xb = sb("xb", [P, 2, CC, N])
        bn = sb("bn1", [P, CC, 2, 6])
        mv = sb("mv1", [P, CC, 2])
        mt = sb("mt1", [P, CC, 2])
        t1 = sb("t11", [P, CC])
        t2 = sb("t12", [P, CC])
        sd = sb("sd1", [P, CC])
        r1 = sb("r11", [P, CC])
        n1 = sb("n11", [P, CC])
        hf = sb("hf", [P, CC, N])
        hh = sb("hh", [P, 2, CC, N], F16)
        hl = sb("hl", [P, 2, CC, N], F16)
        kf = sb("kf", [NP, NB, C])
        ks = sb("ks", [NP, NB, C], F16)
        kq = sb("kq", [NP, NB])
        kn = sb("kn", [NP, NB])
        kr = sb("kr", [NP, NB])
        kh = sb("kh", [NP, NB, C], F16)
        kl = sb("kl", [NP, NB, C], F16)
        vth = sb("vth", [NP, NB, C + 2], F16)
        vtl = sb("vtl", [NP, NB, C + 2], F16)
        vk = sb("vk", [P, CC, C])
        vkh = sb("vkh", [P, CC, C], F32R)
        vkl = sb("vkl", [P, CC, C], F32R)
        km = sb("km", [P, CC])
        kmb = sb("kmb", [P, CC, 32])
        tf = sb("tf", [P, CC, N])
        th = sb("th", [P, CC, N], F32R)
        tl = sb("tl", [P, CC, N], F32R)
        sq = sb("sq", [P, CC, N])
        af = sb("af", [P, CC, N])
        nn = sb("nn", [P, Q])
        ww = sb("ww", [P, Q])
        sf = sb("sf", [P, Q])
        vp = sb("vp", [P, 2, CC, PAD2, PAD2])
        vs = sb("vs", [P, CC, FP, 2, FJ, PAD2], F16)
        vq = sb("vq", [P, CC, FP, 2, FJ, PAD2], F16)
        dq = wf[:, :, :].rearrange("p c n -> p (c n)")[:, 0:CC * N].rearrange("p (c f n) -> p c f n", c=CC, f=FP)
        acc = sb("acc", [P, CC, N])
        yh = sb("yh", [P, CC, N], F16)
        yl = sb("yl", [P, CC, N], F16)
        of = sb("of", [P, CC, N])
        xr = sb("xr", [P, 2, CC, N])

        sl = kc[:, 0:4 * P].rearrange("p (q m) -> p q m", q=4)
        idn = kc[:, 4 * P:4 * P + FC]
        ones, mean_ch, mean_px = kc[:, 5 * P:5 * P + 32], kc[:, 5 * P + 32:5 * P + 64], kc[:, 5 * P + 64:5 * P + 96]
        psum = lambda n: ctx.enter_context(nc.psum_tensor(n, [P, 512], F32))
        pa, pd, pb = [psum(f"pa{k}") for k in range(4)], [psum(f"pd{k}") for k in range(2)], [psum(f"pb{k}") for k in range(2)]
        a_full, a_free = [sem(f"a_full{k}") for k in range(4)], [sem(f"a_free{k}") for k in range(4)]
        d_full, d_free = [sem(f"d_full{k}") for k in range(2)], [sem(f"d_free{k}") for k in range(2)]
        b_full, b_free = [sem(f"b_full{k}") for k in range(2)], [sem(f"b_free{k}") for k in range(2)]
        w_in, w_hi, w_ok, pad_ok, dw_ok, dg_ok, pb_ok = [sem("l1_" + n) for n in (
            "w_in", "w_hi", "w_ok", "pad_ok", "dw_ok", "dg_ok", "pb_ok")]
        xb_in, xr_in, o_out = [[sem(f"{n}{k}") for k in range(2)] for n in ("xb_in", "xr_in", "o_out")]
        bn_ok, mv_ok, sd_ok, rn_ok, hf_ok, hh_ok, hl_ok = [sem(n) for n in ("bn_ok", "mv_ok", "sd_ok", "rn_ok", "hf_ok", "hh_ok", "hl_ok")]
        vt_hi, kv_out, kf_ok, ksq_ok, kq_ok, kn_ok, kx_ok, kh_ok, kl_ok = [sem(n) for n in (
            "vt_hi", "kv_out", "kf_ok", "ksq_ok", "kq_ok", "kn_ok", "kx_ok", "kh_ok", "kl_ok")]
        sp_turn, vh_ok, vl_ok, vd_in, vq_in, dp_ok, ad_in, acc_in = [sem(n) for n in (
            "sp_turn", "vh_ok", "vl_ok", "vd_in", "vq_in", "dp_ok", "ad_in", "acc_in")]
        TURN = 16 * FP
        qr_ok, tf_ok, th_ok, tsq_ok, tl_ok = [sem(n) for n in ("qr_ok", "tf_ok", "th_ok", "tsq_ok", "tl_ok")]
        vk_ok, vkh_ok, kmb_ok, vkl_ok = [sem(n) for n in ("vk_ok", "vkh_ok", "kmb_ok", "vkl_ok")]
        af_ok, asq_ok, nn_ok, ww_ok, fs_ok, sf_ok = [sem(n) for n in ("af_ok", "asq_ok", "nn_ok", "ww_ok", "fs_ok", "sf_ok")]
        y_ok, yh_ok, yl_ok, of_ok, o_ok, dv = [sem(n) for n in ("y_ok", "yh_ok", "yl_ok", "of_ok", "o_ok", "dv")]
        block = ctx.enter_context(nc.Block())

        V, KV, QJ, VK, SS, KZ, AT, JOBS = 0, 4, 11, 15, 17, 18, 19, 23
        A = lambda s, off: (off % 4, (JOBS + 3 - off % 4) // 4 * s + off // 4)
        D = lambda s, off: (off % 2, (5 - off % 2 + 1) // 2 * s + off // 2)

        def BJ(r, off):
            return off % 2, 4 * r + 3 + off // 2 - (max(r - (B - 3), 0) if isinstance(r, int) else 0)

        def stat_job(s, c):
            return c, s if isinstance(s, int) and s < 2 else 4 * s - 6

        def full(eng, sems, job):
            eng.wait_ge(sems[job[0]], job[1] + 1)

        def free(eng, sems, job):
            need(eng, sems[job[0]], job[1])

        def slots(eng, slot, ahead=0):
            slot(0, 0, 0, "first")
            slot(1, 1, 0, "")
            slot(2, 0, 1, "")
            with eng.Fori(1, B // 2 - 1 - ahead) as t:
                slot(2 * t + 1, 1, t, "")
                slot(2 * t + 2, 0, t + 1, "")
            for t in range(B // 2 - 1 - ahead, B // 2 - 1):
                slot(2 * t + 1, 1, t, "")
                slot(2 * t + 2, 0, t + 1, "")
            slot(B - 1, 1, B // 2 - 1, "last")
            slot(B, 0, B // 2, "rest")

        def image(dram, s):
            if isinstance(s, int):
                return dram[s]
            return dram[bass.ds(s, 1)].rearrange("a p c n -> (a p) c n")

        def phases(v):
            return v.rearrange("p f j x -> p j f x")

        def rows_of(v):
            return v.rearrange("p (j f) x -> p j f x", f=FP)

        x1v = x1s.rearrange("b c p n -> b p c n")

        @block.sync
        def _(sp):
            for dst, src in ((wf[:, :, :], lw), (bkb[:, :], rows), (kc[:, :], l1c), (dr[:, :, :], dwc), (bw[:, :, :], dwb)):
                sp.dma_start(dst, src).then_inc(w_in, 16)

            def load(s, par):
                if not (isinstance(s, int) and s < 2):
                    sp.wait_ge(hf_ok, s - 1)
                sp.dma_start(xb[:, par], image(x1v, s)).then_inc(xb_in[par], 16)

            def to_phases(s):
                for c in range(CC):
                    sp.wait_ge(vl_ok, CC * s + c + 1)
                    sp.nop().then_inc(sp_turn, 1)
                    need(sp, vq_in, 16 * (CC * s + c))
                    sp.nop().then_inc(sp_turn, 1)
                    for g in range(FP):
                        sp.dma_start(vdram[c].rearrange("(f p) (g n) -> p f g n", p=FC, g=FP)[:, :, g],
                                     vs[FC * g:FC * g + FC, c].rearrange("p f a j x -> p f (a j x)")).then_inc(vd_in, 16)
                    if c == 0 and not (isinstance(s, int) and s == 0):
                        full(sp, d_full, D(s - 1, 2))
                        sp.nop().then_inc(sp_turn, 1)
                        full(sp, d_full, D(s - 1, 3))
                        sp.nop().then_inc(sp_turn, 1)
                    sp.wait_ge(vd_in, TURN * (CC * s + c + 1))
                    sp.nop().then_inc(sp_turn, 1)
                    sp.dma_start(vq[:, c].rearrange("p g a j x -> p (g a j x)"), vdram[c]).then_inc(vq_in, 16)

            def to_channels(s):
                for c in range(CC):
                    sp.wait_ge(dp_ok, 4 * s + 2 * c + 2)
                    sp.nop().then_inc(sp_turn, 1)
                    need(sp, acc_in, TURN * (CC * s + c))
                    sp.nop().then_inc(sp_turn, 1)
                    for f in range(FP):
                        sp.dma_start(adram[c].rearrange("(g p) (f n) -> p g f n", p=FC, f=FP)[:, :, f],
                                     dq[FC * f:FC * f + FC, c]).then_inc(ad_in, 16)
                    need(sp, y_ok, s)
                    sp.nop().then_inc(sp_turn, 1)
                    sp.wait_ge(ad_in, TURN * (CC * s + c + 1))
                    sp.nop().then_inc(sp_turn, 1)
                    for f in range(FP):
                        sp.dma_start(acc[:, c].rearrange("p (r f x) -> p r f x", f=FP, x=IMG)[:, :, f],
                                     adram[c].rearrange("p (f r x) -> p f r x", f=FP, x=IMG)[:, f]).then_inc(acc_in, 16)

            def slot(s, par, half, kind):
                if not (isinstance(s, int) and s + 2 >= B):
                    load(s + 2, par)
                if kind != "first":
                    r, rp = s - 1, 1 - par
                    rh = half if par else half - 1
                    if not (isinstance(s, int) and s < 3):
                        need(sp, o_out[rp], 16 * rh)
                    sp.dma_start(xr[:, rp], image(x1v, r)).then_inc(xr_in[rp], 16)
                if kind != "rest":
                    to_phases(s)
                    to_channels(s)
                if kind != "first":
                    sp.wait_ge(o_ok, CC * (r + 1))
                    sp.dma_start(image(ov, r), xr[:, rp]).then_inc(o_out[rp], 16)

            load(0, 0)
            load(1, 1)
            slots(sp, slot, 1)
            for k in range(2):
                sp.wait_ge(o_out[k], 16 * (B // 2))

        @block.gpsimd
        def _(pool):
            def norm_low(s, par):
                pool.wait_ge(hh_ok, s + 1)
                for c in range(CC):
                    last = pool.tensor_tensor(hl[:, par, c], hf[:, c], hh[:, par, c], ALU.subtract)
                last.then_inc(hl_ok, 1)

            def v_low(s, par):
                pool.wait_ge(vh_ok, s + 1)
                for c in range(CC):
                    pool.tensor_tensor(phases(vs[:, c, :, 1]), rows_of(vp[:, par, c]), phases(vs[:, c, :, 0]),
                                       ALU.subtract).then_inc(vl_ok, 1)

            def residual(r, rp, rh):
                pool.wait_ge(xr_in[rp], 16 * (rh + 1))
                for c in range(CC):
                    pool.wait_ge(of_ok, 4 * r + 2 * c + 2)
                    pool.tensor_tensor(xr[:, rp, c], xr[:, rp, c], of[:, c], ALU.add).then_inc(o_ok, 1)

            pool.wait_ge(pad_ok, 4)
            norm_low(0, 0)

            def slot(s, par, half, kind):
                if kind != "rest":
                    v_low(s, par)
                if kind in ("first", ""):
                    norm_low(s + 1, 1 - par)
                if kind != "first":
                    residual(s - 1, 1 - par, half if par else half - 1)

            slots(pool, slot)

        @block.scalar
        def _(act):
            def norm_root(s):
                act.wait_ge(mv_ok, 2 * s + 1)
                act.activation(sd[:, :], sd[:, :], ACT.Sqrt, bias=eps).then_inc(sd_ok, 1)

            def norm(s, par):
                act.wait_ge(mv_ok, 2 * s + 2)
                need(act, hl_ok, s)
                for c in range(CC):
                    last = act.activation(hf[:, c], xb[:, par, c], ACT.Identity, scale=r1[:, c:c + 1], bias=n1[:, c:c + 1])
                last.then_inc(hf_ok, 1)

            def norm_high(s, par):
                act.wait_ge(hf_ok, s + 1)
                act.activation(hh[:, par], hf[:, :, :], ACT.Copy).then_inc(hh_ok, 1)

            def v_pixels(s, j):
                job = A(s, KV + j)
                full(act, a_full, job)
                act.activation(vth[:, j, 0:C], pa[job[0]][0:NP, C:2 * C], ACT.Copy, scale=1.0 / WS).then_inc(vt_hi, 1)

            def keys(s):
                act.wait_ge(kf_ok, s + 1)
                act.activation(kf[:, :, :], kf[:, :, :], ACT.Square).then_inc(ksq_ok, 1)
                act.wait_ge(ksq_ok, s + 1)
                for j in range(NB):
                    act.activation(ks[:, j], kf[:, j], ACT.Square, accum_out=kq[:, j:j + 1]).then_inc(kq_ok, 1)
                act.wait_ge(kq_ok, NB * s + NB)
                act.activation(kn[:, :], kq[:, :], ACT.Sqrt).then_inc(kn_ok, 1)

            def keys_high(s):
                act.wait_ge(kx_ok, s + 1)
                act.activation(kh[:, :, :], kf[:, :, :], ACT.Copy).then_inc(kh_ok, 1)

            def values(s, par, before):
                need(act, y_ok, s - 1)
                for c in range(CC):
                    for h in range(2):
                        job = A(s, V + 2 * c + h)
                        full(act, a_full, job)
                        act.activation(vp[:, par, c, 2 + h * HR:2 + h * HR + HR, 2:2 + IMG],
                                       pa[job[0]][:, 0:HALF].rearrange("p (a b) -> p a b", a=HR), ACT.Identity,
                                       scale=1.0 / WS, bias=col[:, 6 + c:7 + c]).then_inc(a_free[job[0]], 1)
                        act.wait_ge(a_free[job[0]], job[1] + 1)
                need(act, vq_in, 16 * CC * s)
                if before:
                    scale(s - 1)
                for c in range(CC):
                    last = act.activation(phases(vs[:, c, :, 0]), rows_of(vp[:, par, c]), ACT.Copy)
                last.then_inc(vh_ok, 1)

            def queries(s):
                for c in range(CC):
                    for h in range(2):
                        job = A(s, QJ + 2 * c + h)
                        full(act, a_full, job)
                        act.activation(tf[:, c, h * HALF:(h + 1) * HALF], pa[job[0]][:, 0:HALF], ACT.Relu,
                                       scale=1.0 / WS, bias=col[:, 4 + c:5 + c]).then_inc(a_free[job[0]], 1)
                        act.wait_ge(a_free[job[0]], job[1] + 1)

            def queries_square(s):
                act.activation(tf[:, :, :], tf[:, :, :], ACT.Square, bias=eps).then_inc(tf_ok, 1)

            def queries_end(s):
                act.wait_ge(tf_ok, s + 1)
                act.activation(th[:, :, :], tf[:, :, :], ACT.Copy).then_inc(th_ok, 1)
                act.activation(sq[:, :, :], tf[:, :, :], ACT.Square).then_inc(tsq_ok, 1)

            def product_high(s):
                for c in range(CC):
                    act.wait_ge(vk_ok, CC * s + c + 1)
                    act.activation(vkh[:, c], vk[:, c], ACT.Copy, scale=1.0 / (KS * N)).then_inc(vkh_ok, 1)
                    act.activation(kmb[:, c], mean_px, ACT.Copy, scale=km[:, c:c + 1]).then_inc(kmb_ok, 1)

            def attention(s):
                full(act, a_full, A(s, SS))
                act.activation(nn[:, :], pa[SS % 4][:, 0:Q], ACT.Sqrt).then_inc(a_free[SS % 4], 1)
                need(act, yl_ok, s)
                for c in range(CC):
                    for h in range(2):
                        job = A(s, AT + 2 * c + h)
                        full(act, a_full, job)
                        act.activation(af[:, c, h * HALF:(h + 1) * HALF], pa[job[0]][:, 0:HALF],
                                       ACT.Copy).then_inc(a_free[job[0]], 1)
                        act.wait_ge(a_free[job[0]], job[1] + 1)
                act.activation(sq[:, :, :], af[:, :, :], ACT.Square).then_inc(asq_ok, 1)

            def scale(s):
                act.wait_ge(ww_ok, s + 1)
                act.activation(ww[:, :], ww[:, :], ACT.Sqrt).then_inc(fs_ok, 1)

            def depthwise(s, c):
                if c == 0:
                    need(act, acc_in, CC * TURN * s)
                for h in range(2):
                    job = D(s, 2 * c + h)
                    full(act, d_full, job)
                    act.activation(dq[:, c, 2 * h:2 * h + 2].rearrange("p g n -> p (g n)"), pd[job[0]][:, 0:HALF],
                                   ACT.Copy).then_inc(d_free[job[0]], 1)
                    act.wait_ge(d_free[job[0]], job[1] + 1)
                act.nop().then_inc(dp_ok, 2)

            def y_high(r, par):
                act.wait_ge(y_ok, r + 1)
                act.activation(yh[:, :, :], af[:, :, :], ACT.Copy).then_inc(yh_ok, 1)

            def project(r):
                need(act, o_ok, CC * r)
                for c in range(CC):
                    for h in range(2):
                        job = BJ(r, 2 + 2 * c + h)
                        full(act, b_full, job)
                        act.activation(of[:, c, h * HALF:(h + 1) * HALF], pb[job[0]][:, 0:HALF], ACT.Identity,
                                       scale=1.0 / WS, bias=pbc[:, c:c + 1]).then_inc(b_free[job[0]], 1)
                        act.wait_ge(b_free[job[0]], job[1] + 1)
                    act.nop().then_inc(of_ok, 2)

            act.wait_ge(w_in, 80)
            act.activation(wh[:, :, :], wf[:, :, :], ACT.Copy, scale=WS).then_inc(w_hi, 1)
            act.wait_ge(pad_ok, 4)
            norm_root(0)
            norm(0, 0)
            norm_high(0, 0)

            def slot(s, par, half, kind):
                live, before = kind != "rest", kind != "first"
                if live:
                    values(s, par, before)
                elif before:
                    scale(s - 1)
                if live:
                    for j in range(NB):
                        v_pixels(s, j)
                    queries(s)
                    keys(s)
                    if kind in ("first", ""):
                        norm_root(s + 1)
                    queries_square(s)
                    depthwise(s, 0)
                    keys_high(s)
                    queries_end(s)
                if kind in ("first", ""):
                    norm(s + 1, 1 - par)
                    norm_high(s + 1, 1 - par)
                if before:
                    y_high(s - 1, 1 - par)
                if live:
                    depthwise(s, 1)
                if live:
                    product_high(s)
                if before:
                    project(s - 1)
                if live:
                    attention(s)

            slots(act, slot)

        @block.vector
        def _(dve):
            chain = Tally(dv)

            def step(ins):
                chain.inc(ins)
                dve.wait_ge(dv, chain.value())

            def moments(s, par, half):
                dve.wait_ge(xb_in[par], 16 * (half + 1))
                for c in range(CC):
                    for h in range(2):
                        last = dve.bn_stats(bn[:, c, h], xb[:, par, c, h * HALF:(h + 1) * HALF])
                step(last)
                dve.nop().then_inc(bn_ok, 1)
                for c in range(CC):
                    last = dve.bn_aggr(mv[:, c], bn[:, c])
                step(last)
                step(dve.tensor_tensor(t1[:, :], mv[:, :, 0], mv[:, :, 0], ALU.mult))
                dve.tensor_tensor(mv[:, :, 1], mv[:, :, 1], t1[:, :], ALU.add).then_inc(rn_ok, 1)

            def statistics(s):
                for c in range(CC):
                    job = stat_job(s, c)
                    full(dve, b_full, job)
                    dve.tensor_copy(mt[:, c], pb[job[0]][:, 0:2]).then_inc(b_free[job[0]], 1)
                    dve.wait_ge(b_free[job[0]], job[1] + 1)
                step(dve.tensor_tensor(t2[:, :], mt[:, :, 0], mt[:, :, 0], ALU.mult))
                step(dve.tensor_tensor(sd[:, :], mt[:, :, 1], t2[:, :], ALU.subtract))
                dve.tensor_scalar(sd[:, :], sd[:, :], 0.0, None, ALU.max).then_inc(mv_ok, 1)

            def statistics_end(s):
                dve.wait_ge(sd_ok, s + 1)
                step(dve.reciprocal(r1[:, :], sd[:, :]))
                dve.scalar_tensor_tensor(n1[:, :], mt[:, :, 0], -1.0, r1[:, :], ALU.mult, ALU.mult).then_inc(mv_ok, 1)

            def pixels(s, j):
                job = A(s, KV + j)
                dve.wait_ge(vt_hi, NB * s + j + 1)
                dve.scalar_tensor_tensor(kf[:, j], pa[job[0]][0:NP, 0:C], 1.0 / WS, bkb[0:NP, 0:C], ALU.mult, ALU.add)
                dve.scalar_tensor_tensor(vtl[:, j, 0:C], pa[job[0]][0:NP, C:2 * C], 1.0 / WS, vth[:, j, 0:C],
                                         ALU.mult, ALU.subtract).then_inc(a_free[job[0]], 1)
                if j == NB - 1:
                    dve.wait_ge(a_free[job[0]], job[1] + 1)

            def keys(s):
                dve.tensor_scalar(kf[:, :, :], kf[:, :, :], 0.0, EPS, ALU.max, ALU.add).then_inc(kf_ok, 1)

            def keys_scale(s):
                dve.wait_ge(kn_ok, s + 1)
                step(dve.tensor_scalar(kr[:, :], kn[:, :], 1e-12, 1.0 / KS, ALU.max, ALU.mult))
                step(dve.reciprocal(kr[:, :], kr[:, :]))
                dve.tensor_tensor(kf[:, :, :], kf[:, :, :], kr[:, :].unsqueeze(2).to_broadcast([NP, NB, C]),
                                  ALU.mult).then_inc(kx_ok, 1)

            def keys_low(s):
                dve.wait_ge(kh_ok, s + 1)
                dve.tensor_tensor(kl[:, :, :], kf[:, :, :], kh[:, :, :], ALU.subtract).then_inc(kl_ok, 1)

            def product(s):
                for c in range(CC):
                    job = A(s, VK + c)
                    full(dve, a_full, job)
                    bank = pa[job[0]]
                    step(dve.tensor_copy(km[:, c:c + 1], bank[:, C:C + 1]))
                    dve.scalar_tensor_tensor(vk[:, c], bkb[:, C:2 * C], km[:, c:c + 1], bank[:, 0:C],
                                             ALU.mult, ALU.add).then_inc(vk_ok, 1)
                    dve.wait_ge(vk_ok, CC * s + c + 1)
                    dve.nop().then_inc(a_free[job[0]], 1)

            def product_low(s):
                for c in range(CC):
                    dve.wait_ge(vkh_ok, CC * s + c + 1)
                    dve.scalar_tensor_tensor(vkl[:, c], vk[:, c], 1.0 / (KS * N), vkh[:, c],
                                             ALU.mult, ALU.subtract).then_inc(vkl_ok, 1)

            def query_low(s):
                dve.wait_ge(th_ok, s + 1)
                dve.tensor_tensor(tl[:, :, :], tf[:, :, :], th[:, :, :], ALU.subtract).then_inc(tl_ok, 1)

            def taps(s, par, first, n):
                for t in range(first, min(first + n, VT)):
                    k, c = TAP_ORDER[t]
                    if k == V_TAPS[0]:
                        dve.wait_ge(acc_in, TURN * (CC * s + c + 1))
                    else:
                        before = TAP_ORDER.index((V_TAPS[V_TAPS.index(k) - 1], c))
                        dve.wait_ge(dv, chain.value() - (t - before - 1))
                    dy, dx = divmod(k, KW)
                    whole = acc[:, c].rearrange("p (a b) -> p a b", a=IMG)
                    chain.inc(dve.scalar_tensor_tensor(whole, vp[:, par, c, dy:dy + IMG, dx:dx + IMG], dw[:, c, k:k + 1],
                                                       whole, ALU.mult, ALU.add))

            def scaled(r, par):
                for h in range(2):
                    job = BJ(r, h)
                    full(dve, b_full, job)
                    for c in range(CC):
                        part = af[:, c, h * HALF:(h + 1) * HALF]
                        last = dve.scalar_tensor_tensor(part, part, col[:, 8 + c:9 + c], pb[job[0]][:, 0:HALF],
                                                        ALU.mult, ALU.mult)
                    last.then_inc(b_free[job[0]], 1)
                dve.wait_ge(b_free[1], BJ(r, 1)[1] + 1)
                dve.wait_ge(dv, chain.value())
                y = af[:, :, :].rearrange("p c n -> p (c n)")
                dve.scalar_tensor_tensor(y, acc[:, :, :].rearrange("p c n -> p (c n)"), 1.0 / WS, y,
                                         ALU.mult, ALU.add).then_inc(y_ok, 1)

            def y_low(r, par):
                dve.wait_ge(yh_ok, r + 1)
                dve.tensor_tensor(yl[:, :, :], af[:, :, :], yh[:, :, :], ALU.subtract).then_inc(yl_ok, 1)

            def scale(s):
                full(dve, a_full, A(s, KZ))
                dve.wait_ge(a_free[SS % 4], A(s, SS)[1] + 1)
                step(dve.tensor_scalar(nn[:, :], nn[:, :], 1e-12, EPS, ALU.max, ALU.mult))
                dve.tensor_tensor(ww[:, :], nn[:, :], pa[KZ % 4][:, 0:Q], ALU.add).then_inc(a_free[KZ % 4], 1)
                dve.wait_ge(a_free[KZ % 4], A(s, KZ)[1] + 1)
                step(dve.scalar_tensor_tensor(nn[:, :], ww[:, :], EPS, ww[:, :], ALU.mult, ALU.mult))

            def scale_end(s):
                job = D(s, 4)
                full(dve, d_full, job)
                dve.tensor_tensor(ww[:, :], nn[:, :], pd[job[0]][:, 0:Q], ALU.add).then_inc(d_free[job[0]], 1)
                dve.wait_ge(d_free[job[0]], job[1] + 1)
                dve.nop().then_inc(ww_ok, 1)

            def scale_inverse(s):
                dve.wait_ge(fs_ok, s + 1)
                dve.reciprocal(sf[:, :], ww[:, :]).then_inc(sf_ok, 1)

            dve.memset(vp[:, :, :, :, :], 0.0).then_inc(pad_ok, 1)
            dve.nop().then_inc(pad_ok, 1)
            dve.memset(vth[:, :, C:C + 2], 1.0).then_inc(pad_ok, 1)
            dve.memset(vtl[:, :, C:C + 2], 0.0).then_inc(pad_ok, 1)
            dve.wait_ge(w_in, 80)
            step(dve.tensor_scalar(dw[:, :, :], dr[:, :, :], WS, None, ALU.mult))
            step(dve.tensor_scalar(bw[:, :, :], bw[:, :, :], WS, None, ALU.mult))
            dve.wait_ge(w_hi, 1)
            dve.scalar_tensor_tensor(wl[:, :, :].rearrange("p c n -> p (c n)"), wf[:, :, :].rearrange("p c n -> p (c n)"), WS,
                                     wh[:, :, :].rearrange("p c n -> p (c n)"), ALU.mult, ALU.subtract).then_inc(w_ok, 1)
            dve.wait_ge(pb_ok, 1)
            for c in range(CC):
                dve.tensor_tensor(pbc[:, c:c + 1], pb[c][:, 0:1], col[:, 12 + c:13 + c], ALU.add).then_inc(dw_ok, 1)
            moments(0, 0, 0)
            statistics(0)
            statistics_end(0)
            moments(1, 1, 0)
            dve.wait_ge(w_ok, 1)
            for n in range(CC * FP):
                m = bdm.rearrange("p (m c) -> p m c", c=FC)
                step(dve.tensor_tensor(m, bw[:, n].unsqueeze(2).to_broadcast([P, NM * FP, FC]),
                                       idn.unsqueeze(1).to_broadcast([P, NM * FP, FC]), ALU.mult))
                step(dve.tensor_copy(bmh[:, n].rearrange("p m c -> p (m c)"), bdm))
                step(dve.tensor_tensor(bml[:, n].rearrange("p m c -> p (m c)"), bdm, bmh[:, n].rearrange("p m c -> p (m c)"),
                                       ALU.subtract))
            dve.nop().then_inc(dg_ok, 1)

            def slot(s, par, half, kind):
                live, before = kind != "rest", kind != "first"
                r, rp = s - 1, 1 - par

                def rest(first, n):
                    if before:
                        taps(r, rp, first, n)

                if before:
                    scale_end(r)
                rest(EARLY, 3)
                if before and not live:
                    scale_inverse(r)
                if live:
                    for j in range(NB):
                        if before and j == 2:
                            scale_inverse(r)
                        pixels(s, j)
                        if j % 2:
                            rest(EARLY + 3 + j // 2, 1)
                    keys(s)
                    if kind in ("first", ""):
                        statistics(s + 1)
                    rest(EARLY + 6, 4)
                    keys_scale(s)
                    rest(EARLY + 10, 2)
                    keys_low(s)
                    rest(EARLY + 12, VT)
                    if kind in ("first", ""):
                        statistics_end(s + 1)
                else:
                    rest(EARLY + 3, VT)
                if before:
                    scaled(r, rp)
                if live:
                    query_low(s)
                if before:
                    y_low(r, rp)
                if live:
                    product(s)
                    product_low(s)
                if live:
                    if not (isinstance(s, int) and s + 2 >= B):
                        moments(s + 2, par, half + 1)
                    taps(s, par, 0, FIRST)
                    scale(s)
                    taps(s, par, FIRST, EARLY - FIRST)

            slot(0, 0, 0, "first")
            slot(1, 1, 0, "")
            slot(2, 0, 1, "")
            with dve.Fori(1, B // 2 - 2) as t:
                chain.loop(t - 1, DV_LOOP)
                slot(2 * t + 1, 1, t, "")
                slot(2 * t + 2, 0, t + 1, "")
            chain.end(B // 2 - 3)
            slot(B - 3, 1, B // 2 - 2, "")
            slot(B - 2, 0, B // 2 - 1, "")
            slot(B - 1, 1, B // 2 - 1, "last")
            slot(B, 0, B // 2, "rest")

        @block.tensor
        def _(pe):
            def products(bank, terms, sync=None):
                for n, (w, m) in enumerate(terms):
                    last = pe.matmul(bank, w, m, start=(n == 0), stop=(n == len(terms) - 1))
                if sync is not None:
                    last.then_inc(sync, 1)

            def pairs(hi_w, lo_w, hi_m, lo_m):
                return ((hi_w, hi_m), (hi_w, lo_m), (lo_w, hi_m))

            def keys_values(s, par):
                for j in range(NB):
                    job = A(s, KV + j)
                    free(pe, a_free, job)
                    px = slice(NP * j, NP * j + NP)
                    products(pa[job[0]][0:NP, :], [t for c in range(CC) for t in pairs(
                        hh[:, par, c, px], hl[:, par, c, px], wh[:, c, C:3 * C], wl[:, c, C:3 * C])], a_full[job[0]])

            def channels(s, par, first, w0, blocks=(0, 1, 2, 3)):
                for m in range(CC):
                    for h in range(2):
                        if 2 * m + h not in blocks:
                            continue
                        job = A(s, first + 2 * m + h)
                        free(pe, a_free, job)
                        px, wc = slice(HALF * h, HALF * h + HALF), slice(w0 + P * m, w0 + P * m + P)
                        products(pa[job[0]][:, 0:HALF], [t for c in range(CC) for t in pairs(
                            wh[:, c, wc], wl[:, c, wc], hh[:, par, c, px], hl[:, par, c, px])], a_full[job[0]])

            def product(s):
                pe.wait_ge(kl_ok, s + 1)
                for c in range(CC):
                    job = A(s, VK + c)
                    free(pe, a_free, job)
                    ch = slice(P * c, P * c + P)
                    products(pa[job[0]][:, 0:C + 1], [t for j in range(NB) for t in pairs(
                        kh[:, j, ch], kl[:, j, ch], vth[:, j, 0:C + 1], vtl[:, j, 0:C + 1])], a_full[job[0]])

            def quarters(banks, sem_full, sem_free, job, weight, moving):
                free(pe, sem_free, job)
                for q in range(4):
                    for c in range(CC):
                        last = pe.matmul(banks[job[0]][32 * q:32 * q + 32, 0:Q], weight(c), moving[:, c, Q * q:Q * q + Q],
                                         start=(c == 0), stop=(c == CC - 1))
                last.then_inc(sem_full[job[0]], 1)

            def attention(s):
                for m in range(CC):
                    for h in range(2):
                        job = A(s, AT + 2 * m + h)
                        free(pe, a_free, job)
                        px, ch = slice(HALF * h, HALF * h + HALF), slice(P * m, P * m + P)
                        products(pa[job[0]][:, 0:HALF], [t for c in range(CC) for t in pairs(
                            vkh[:, c, ch], vkl[:, c, ch], th[:, c, px], tl[:, c, px])], a_full[job[0]])

            def depthwise(s, c, h):
                job = D(s, 2 * c + h)
                free(pe, d_free, job)
                pe.wait_ge(vq_in, 16 * (CC * s + c + 1))
                for k in range(2):
                    g = 2 * h + k
                    terms = []
                    for n in range(NM):
                        dx, b = PX[n // FB], n % FB
                        high, low = [vq[:, c, g, a, b:b + FO, dx:dx + IMG] for a in range(2)]
                        terms += pairs(bmh[:, FP * c + g, n], bml[:, FP * c + g, n], high, low)
                    for n, (w, m) in enumerate(terms):
                        last = pe.matmul(pd[job[0]][:, k * FO * IMG:(k + 1) * FO * IMG], w, m, start=(n == 0 and k == 0),
                                         stop=(n == len(terms) - 1), skip_group_check=True)
                last.then_inc(d_full[job[0]], 1)

            def statistics(s):
                pe.wait_ge(rn_ok, s + 1)
                for c in range(CC):
                    job = stat_job(s, c)
                    free(pe, b_free, job)
                    products(pb[job[0]][:, 0:2], [(gavg, mv[:, c])], b_full[job[0]])

            def spread(r):
                pe.wait_ge(sf_ok, r + 1)
                for h in range(2):
                    job = BJ(r, h)
                    free(pe, b_free, job)
                    for k in range(2):
                        last = pe.matmul(pb[job[0]][:, Q * k:Q * k + Q], sl[:, 2 * h + k], sf[:, :],
                                         start=(k == 0), stop=True, skip_group_check=True)
                    last.then_inc(b_full[job[0]], 1)

            def project(r):
                pe.wait_ge(yl_ok, r + 1)
                for m in range(CC):
                    for h in range(2):
                        job = BJ(r, 2 + 2 * m + h)
                        free(pe, b_free, job)
                        px, wc = slice(HALF * h, HALF * h + HALF), slice(3 * C + P * m, 3 * C + P * m + P)
                        products(pb[job[0]][:, 0:HALF], [t for c in range(CC) for t in pairs(
                            wh[:, c, wc], wl[:, c, wc], yh[:, c, px], yl[:, c, px])], b_full[job[0]])

            pe.wait_ge(w_in, 80)
            for m in range(CC):
                products(pb[m][:, 0:1], [(wf[:, c, 3 * C + P * m:3 * C + P * m + P], col[:, 10 + c:11 + c])
                                         for c in range(CC)], pb_ok if m else None)
            pe.wait_ge(dw_ok, 2)
            statistics(0)
            pe.wait_ge(w_ok, 1)

            def slot(s, par, half, kind):
                live, before = kind != "rest", kind != "first"
                if live:
                    pe.wait_ge(hl_ok, s + 1)
                    channels(s, par, V, 2 * C, (0, 1))
                if before:
                    pe.wait_ge(asq_ok, s)
                    quarters(pd, d_full, d_free, D(s - 1, 4), lambda c: mean_ch, sq)
                if live:
                    channels(s, par, V, 2 * C, (2, 3))
                    keys_values(s, par)
                if kind in ("first", ""):
                    statistics(s + 1)
                if live:
                    channels(s, par, QJ, 0)
                if before:
                    spread(s - 1)
                if live:
                    if kind == "first":
                        pe.wait_ge(dg_ok, 1)
                    depthwise(s, 0, 0)
                    depthwise(s, 0, 1)
                    depthwise(s, 1, 0)
                    depthwise(s, 1, 1)
                    product(s)
                    pe.wait_ge(tsq_ok, s + 1)
                    quarters(pa, a_full, a_free, A(s, SS), lambda c: ones, sq)
                if before:
                    project(s - 1)
                if live:
                    pe.wait_ge(kmb_ok, CC * s + CC)
                    quarters(pa, a_full, a_free, A(s, KZ), lambda c: kmb[:, c], tf)
                    pe.wait_ge(tl_ok, s + 1)
                    pe.wait_ge(vkl_ok, CC * s + CC)
                    attention(s)

            slots(pe, slot)


_VECTORS = ["L0_conv_bias", "L1_conv_qkv_b", "L1_conv_qkv_b", "L1_conv_norm_w", "L1_conv_dwc_b", "L1_conv_proj_b"]
_FIRST = [0, 0, 2 * C, 0, 0, 0]


def _constants(np):
    group = np.kron(np.eye(P // GN), np.full((GN, GN), 1.0 / GN)).astype(np.float32)
    mask = np.tile(np.eye(JB) * GSC, (NE, 1)).astype(np.float32)
    l1c = np.zeros((P, 6 * P), np.float32)
    for q in range(4):
        l1c[32 * q, q * P:(q + 1) * P] = 1.0
    l1c[:, 4 * P:4 * P + FC] = np.tile(np.eye(FC), (FP, 1))
    for k, v in enumerate((1.0, 1.0 / C, 1.0 / (KS * N))):
        l1c[:, 5 * P + 32 * k:5 * P + 32 * k + 32] = v
    return group, mask, l1c


def kernel(**inputs):
    import numpy as np
    import concourse.bacc as bacc
    from concourse.bass_utils import run_bass_kernel_spmd

    a = {k: np.asarray(v) for k, v in inputs.items()}
    group, mask, l1c = _constants(np)
    rw = a["L0_conv_route_w"].reshape(NE, CC, P).transpose(2, 1, 0)
    route = np.concatenate([np.repeat(rw, JB, axis=2).reshape(P, CC * P), mask], axis=1)
    wmix = a["L0_conv_weight"].reshape(2, P // JB, JB, CC, P, 9, NE).transpose(0, 3, 5, 6, 2, 1, 4).reshape(3 * TR, P, P * P // JB)
    cols = [np.full((P, 1), EPS, np.float32), np.repeat(a["L0_conv_route_b"], JB).reshape(P, 1)]
    for name, first in zip(_VECTORS, _FIRST):
        cols.append(a[name][first:first + C].reshape(CC, P).T)
    lw = np.concatenate([a["L1_conv_qkv_w"], a["L1_conv_proj_w"]], axis=0).T.reshape(CC, P, 4 * C).transpose(1, 0, 2)
    data = {
        "x": a["x"], "route": route, "wmix": wmix, "consts": group, "cols": np.concatenate(cols, axis=1), "lw": lw,
        "rows": np.broadcast_to(a["L1_conv_qkv_b"][C:3 * C], (P, 2 * C)), "l1c": l1c,
        "dwc": a["L1_conv_dwc_w"].reshape(CC, P, TAPS).transpose(1, 0, 2),
    }
    taps = a["L1_conv_dwc_w"].reshape(CC * FP, FC, KW, KW)
    dwb = np.zeros((FP, FC, CC * FP, len(PX), FB, FP), np.float32)
    for fi in range(FP):
        for b in range(FB):
            for fo in range(FP):
                dy = FP * b + fi - fo
                if 0 <= dy < KW:
                    dwb[fi, :, :, :, b, fo] = taps[:, :, dy, list(PX)].transpose(1, 0, 2)
    data["dwb"] = dwb.reshape(P, CC * FP, len(PX) * FB * FP)
    nc = bacc.Bacc("TRN2", target_bir_lowering=False, num_devices=1)
    data = {k: np.ascontiguousarray(v) for k, v in data.items()}
    args = {k: nc.dram_tensor(f"in_{k}", v.shape, F32, kind="ExternalInput").ap() for k, v in data.items()}
    wpair = nc.dram_tensor("wpair", (2, PH, CC * 3, P, 2 * P * P // JB), F16).ap()
    vdram = nc.dram_tensor("vdram", (CC, P, 2 * FP * FJ * PAD2), F16).ap()
    adram = nc.dram_tensor("adram", (CC, P, N), F32).ap()
    x1s = nc.dram_tensor("x1s", (B, CC, P, N), F32).ap()
    out = nc.dram_tensor("out", (B, C, IMG, IMG), F32, kind="ExternalOutput").ap()
    mk_conv_preact(nc, wpair=wpair, x1s=x1s, vdram=vdram, adram=adram, out=out, **args)
    r = run_bass_kernel_spmd(nc, [{f"in_{k}": v for k, v in data.items()}], core_ids=[0])
    return r.results[0]["out"]
```
